# Optimizing a Trainium2 kernel written in Bass

```python
import numpy as np
import jax
import jax.numpy as jnp

def _softmax(x, axis=-1):
    return jax.nn.softmax(x, axis=axis)

def _gelu(x):
    return jax.nn.gelu(x, approximate=True)

def _silu(x):
    return jax.nn.silu(x)

def _sigmoid(x):
    return jax.nn.sigmoid(x)

def _layernorm(x, axis=-1, eps=1e-05):
    m = jnp.mean(x, axis=axis, keepdims=True)
    v = jnp.var(x, axis=axis, keepdims=True)
    return (x - m) / jnp.sqrt(v + eps)

def _scatter_add(tgt, idx, src, axis=0):
    return tgt.at[idx].add(src)

def _segment_sum(src, seg, n):
    return jax.ops.segment_sum(src, seg, n)
kernel_name = 'mk_adj_resnorm_d2_adj_r2_29b0ca'

def setup_inputs(seed: int=0):
    np.random.seed(seed)
    _w = jnp.asarray

    def _rec_inputs():
        import jax
        import jax.numpy as jnp
        _gk = jax.random.key(seed)
        x = -0.000929 + 1 * jax.random.normal(jax.random.fold_in(_gk, 1), (4096, 128), jnp.float32)
        _a = jax.random.bernoulli(jax.random.fold_in(_gk, 2), 0.000488281, (4096, 4096))
        _a = jnp.logical_or(_a, jnp.swapaxes(_a, -1, -2))
        _a = jnp.logical_or(_a, jnp.eye(4096, dtype=bool))
        _af = _a.astype(jnp.float32)
        adj = _af
        return (x, adj)
    x, adj = _rec_inputs()

    def _L0_gnn_setup():
        import jax, jax.numpy as jnp
        import numpy as np
        N = 2048
        IN_F = 128
        OUT_F = 128
        H = 4
        FH = OUT_F // H
        ALPHA = 0.2
        DENSITY = 0.01
        key = jax.random.key(seed)
        k1, k2, k3, k4 = jax.random.split(key, 4)
        h = jax.random.normal(k1, (N, IN_F), dtype=jnp.float32)
        adj = (jax.random.uniform(k2, (N, N)) < DENSITY).astype(jnp.float32)
        adj = adj.at[jnp.arange(N), jnp.arange(N)].set(1.0)
        W = jax.random.normal(k3, (IN_F, H * FH), dtype=jnp.float32) / np.sqrt(IN_F)
        a = jax.random.normal(k4, (H, 2 * FH), dtype=jnp.float32) * 0.1
        return {'h': h, 'adj': adj, 'W': W, 'a': a}
    _L0_gnn_all = _L0_gnn_setup()
    _L0_gnn_in = {k: v for k, v in _L0_gnn_all.items() if k in ('W', 'a')}
    del _L0_gnn_all

    def _L1_gnn_setup():
        import jax, jax.numpy as jnp
        import numpy as np
        N = 4096
        D = 128
        L = 3

        def _cxin_conv(x, a, eps, W, b):
            ax = a @ x
            h = ax + (1.0 + eps[0]) * ax
            for i in range(L):
                h = jax.nn.relu(h @ W[i].T + b[i])
            return h
        key = jax.random.key(seed)
        ks = jax.random.split(key, 8)
        s = 1.0 / np.sqrt(D)
        return {'x1': jax.random.normal(ks[0], (N, D), jnp.float32), 'x2': jax.random.normal(ks[1], (N, D), jnp.float32), 'G1': jax.random.uniform(ks[2], (N, N), jnp.float32), 'G2': jax.random.uniform(ks[3], (N, N), jnp.float32), 'eps1': jnp.zeros((1,), jnp.float32), 'eps2': jnp.zeros((1,), jnp.float32), 'W1': jax.random.normal(ks[4], (L, D, D), jnp.float32) * s, 'b1': jnp.zeros((L, D), jnp.float32), 'W2': jax.random.normal(ks[5], (L, D, D), jnp.float32) * s, 'b2': jnp.zeros((L, D), jnp.float32), 'Wm': jax.random.normal(ks[6], (D, 2 * D), jnp.float32) * (1.0 / np.sqrt(2 * D)), 'bm': jnp.zeros((D,), jnp.float32)}
    _L1_gnn_all = _L1_gnn_setup()
    _L1_gnn_in = {k: v for k, v in _L1_gnn_all.items() if k in ('x2', 'eps1', 'eps2', 'W1', 'b1', 'W2', 'b2', 'Wm', 'bm')}
    del _L1_gnn_all
    return {'x': x, 'adj': adj, 'L0_gnn_W': _L0_gnn_in['W'], 'L0_gnn_a': _L0_gnn_in['a'], 'L1_gnn_x2': _L1_gnn_in['x2'], 'L1_gnn_eps1': _L1_gnn_in['eps1'], 'L1_gnn_eps2': _L1_gnn_in['eps2'], 'L1_gnn_W1': _L1_gnn_in['W1'], 'L1_gnn_b1': _L1_gnn_in['b1'], 'L1_gnn_W2': _L1_gnn_in['W2'], 'L1_gnn_b2': _L1_gnn_in['b2'], 'L1_gnn_Wm': _L1_gnn_in['Wm'], 'L1_gnn_bm': _L1_gnn_in['bm']}

def reference(x, adj, L0_gnn_W, L0_gnn_a, L1_gnn_x2, L1_gnn_eps1, L1_gnn_eps2, L1_gnn_W1, L1_gnn_b1, L1_gnn_W2, L1_gnn_b2, L1_gnn_Wm, L1_gnn_bm):
    import jax
    import jax.numpy as jnp

    def _L0_gnn_ref(h, adj, W, a):
        import jax, jax.numpy as jnp
        import numpy as np
        N = 2048
        IN_F = 128
        OUT_F = 128
        H = 4
        FH = OUT_F // H
        ALPHA = 0.2
        DENSITY = 0.01
        n = h.shape[0]
        hp = (h @ W).reshape(n, H, FH)
        a_src, a_dst = (a[:, :FH], a[:, FH:])
        s = jnp.einsum('nhf,hf->hn', hp, a_src)
        d = jnp.einsum('nhf,hf->hn', hp, a_dst)
        e = jax.nn.leaky_relu(s[:, :, None] + d[:, None, :], ALPHA)
        e = jnp.where(adj[None, :, :] > 0, e, -jnp.inf)
        attn = jax.nn.softmax(e, axis=2)
        out = jnp.einsum('hij,jhf->ihf', attn, hp).reshape(n, H * FH)
        return jax.nn.elu(out)

    def _L1_gnn_ref(x1, x2, G1, G2, eps1, eps2, W1, b1, W2, b2, Wm, bm):
        import jax, jax.numpy as jnp
        import numpy as np
        N = 4096
        D = 128
        L = 3

        def _cxin_conv(x, a, eps, W, b):
            ax = a @ x
            h = ax + (1.0 + eps[0]) * ax
            for i in range(L):
                h = jax.nn.relu(h @ W[i].T + b[i])
            return h
        out1 = _cxin_conv(x1, G1, eps1, W1, b1)
        out2 = _cxin_conv(x2, G2, eps2, W2, b2)
        merged = jnp.concatenate((out1, out2), axis=1)
        return merged @ Wm.T + bm
    x = _layernorm(x + _L0_gnn_ref(x, adj, L0_gnn_W, L0_gnn_a), axis=-1)
    x = _layernorm(x + _L1_gnn_ref(x, L1_gnn_x2, adj, adj, L1_gnn_eps1, L1_gnn_eps2, L1_gnn_W1, L1_gnn_b1, L1_gnn_W2, L1_gnn_b2, L1_gnn_Wm, L1_gnn_bm), axis=-1)
    return x

_drawn_inputs = setup_inputs


def setup_inputs(seed=0):
    import zlib

    import numpy as np

    out = dict(_drawn_inputs(seed))
    spreads = {'L1_gnn_b1': (0.0, 0.1), 'L1_gnn_b2': (0.0, 0.1), 'L1_gnn_bm': (0.0, 0.1)}
    factors = {}
    for name, (base, spread) in spreads.items():
        noise = np.random.default_rng([zlib.crc32(name.encode()), seed]).standard_normal(out[name].shape)
        drawn = base * np.exp(spread * noise) if base else spread * noise
        out[name] = jnp.asarray(drawn.astype(out[name].dtype))
    for name, factor in factors.items():
        out[name] = (out[name] * factor).astype(out[name].dtype)
    return out
```

```python
from contextlib import ExitStack

import concourse.bass as bass
from concourse import mybir

F32 = mybir.dt.float32
F16 = mybir.dt.float16
F8 = mybir.dt.float8e4
U8 = mybir.dt.uint8
I32 = mybir.dt.int32
ALU = mybir.AluOpType
ACT = mybir.ActivationFunctionType
X = mybir.AxisListType.X
RMAX = bass.bass_isa.ReduceOp.max

P = 128
Q = 32
NB = P // Q
K = 4
FP8_ONE = 56.0
STEP_GAIN = 2.0 ** 60
SPLIT = 2.0 ** 11
HP_TOP = 2.0 ** 13
Y_GAIN = 2.0 ** 10
RING = 4
ACT_STEPS = 10
SLOPE = 0.2
LN_EPS = 1e-5


def gat_gin_resnorm_kernel(nc, x, adj, w, a, x2, eps1, eps2, w1, b1, w2, b2, wm, bm, out):
    N, F = x.shape
    H, FH = a.shape[0], a.shape[1] // 2
    NT = N // P
    NC = NT // K
    CH = K * P
    JB = N // NB
    G = FH + 1
    HB = 4 * G
    ACC = H * HB + H * 2 * G
    BANK0 = 3 * HB
    L = w1.shape[0]

    with ExitStack() as ctx:
        def sb(name, shape, dt):
            return ctx.enter_context(nc.sbuf_tensor(name, shape, dt))

        def sem(name):
            return ctx.enter_context(nc.semaphore(name))

        s_dram = nc.dram_tensor("s_rows", [H, N], F32).ap()

        xs = sb("xs", [P, NT, F], F32)
        gat = sb("gat", [P, NT, F], F32)
        hv = sb("hv", [P, NT, H, HB], F16)
        rows = sb("rows", [P, 2, NB, JB], F32)
        mask = sb("mask", [P, 2, NB * JB], U8)
        maskT = sb("maskT", [P, 2, NC, CH], I32)
        ring = sb("ring", [P, RING, H, CH], I32)
        s_all = sb("s_all", [P, 2, H, CH], F32)
        sums = sb("sums", [P, K, ACC], F32)
        ident = sb("ident", [P, P], F32)
        wext = sb("wext", [P, F + 2 * H], F32)
        ds = sb("ds", [P, NT, 2 * H], F32)
        dneg = sb("dneg", [P, NT, H], F32)
        dbig = sb("dbig", [P, NT, H], F32)
        uw = sb("uw", [P, 2, NT, H], F32)
        top = sb("top", [P, H + 1], F32)
        topall = sb("topall", [P, H + 1], F32)
        hscale = sb("hscale", [P, 1], F32)
        rden = sb("rden", [P, K, H], F32)
        x2top = sb("x2top", [P, 4], F32)
        wt = sb("wt", [P, 2 * L + 2, P], F32)
        bias = sb("bias", [P, 2 * L], F32)
        bm_all = sb("bm_all", [P, F], F32)
        gain = sb("gain", [P, 2], F32)
        eps_all = sb("eps_all", [P, 2], F32)
        mean = sb("mean", [P, NT], F32)
        var = sb("var", [P, NT], F32)
        std = sb("std", [P, NT], F32)
        rstd = sb("rstd", [P, NT], F32)
        ps = ctx.enter_context(nc.psum_tensor("ps", [P, 8, 512], F32))

        flat_ring = ring[:].rearrange("p r h i -> p (r h i)").bitcast(F32)
        xT = flat_ring[:, 0:N]
        wraw = flat_ring[:, N:N + (2 * L + 2) * P].rearrange("p (l n) -> p l n", n=P)
        t_a = flat_ring[:, 0:NT * F].rearrange("p (t f) -> p t f", f=F)
        t_b = flat_ring[:, NT * F:2 * NT * F].rearrange("p (t f) -> p t f", f=F)
        s_rows = s_all[:].rearrange("p r h i -> p (r h i)")[0:H, :]
        flat_sums = sums[:].rearrange("p t n -> p (t n)")
        part = flat_sums[:, 0:2 * NT * G].rearrange("p (r t g) -> p r t g", r=2, g=G)
        a_all = flat_sums[:, 2 * NT * G:2 * NT * G + H * 2 * FH].rearrange("p (h f) -> p h f", h=H)
        vz = flat_sums[:, ACC * K - 2 * NT * H:ACC * K].rearrange("p (q t h) -> p q t h", q=2, h=H)
        yx = hv[:].rearrange("p t h n -> p (t h n)")[:, 0:4 * NT * F].rearrange(
            "p (q t f) -> p q t f", q=4, f=F)
        hid = s_all[:].rearrange("p r h i -> p (r h) i")
        res = flat_sums[:, 0:3 * K * F].rearrange("p (r k f) -> p r k f", r=3, f=F)

        ring8 = ring[:].rearrange("p r h i -> p (r h i)").bitcast(U8).rearrange(
            "p (r h i k) -> p r h i k", r=RING, h=H, k=K)
        ringf8 = ring[:].rearrange("p r h i -> p (r h i)").bitcast(F8).rearrange(
            "p (r h i k) -> p r h i k", r=RING, h=H, k=K)
        maskTf8 = maskT[:].rearrange("p r c i -> p (r c i)").bitcast(F8).rearrange(
            "p (r c i k) -> p r c i k", r=2, c=NC, k=K)

        x_v = x.rearrange("(b c w k) f -> b w c (k f)", b=NB, c=NC, w=Q)
        x2_v = x2.rearrange("(b c w k) f -> b w c (k f)", b=NB, c=NC, w=Q)
        out_v = out.rearrange("(b c w k) f -> c b w (k f)", b=NB, c=NC, w=Q)
        adj_v = adj.rearrange("(B c w k) (b j) -> c k b w B j", B=NB, c=NC, w=Q, b=NB)
        s_v = s_dram.rearrange("h (c i) -> c h i", i=CH)

        x_landed = sem("x_landed")
        w_landed = sem("w_landed")
        gin_w_landed = sem("gin_w_landed")
        x2_landed = sem("x2_landed")
        adj_landed = [sem(f"adj_landed{r}") for r in range(2)]
        s_stored = sem("s_stored")
        s_landed = [sem(f"s_landed{r}") for r in range(2)]
        out_stored = sem("out_stored")
        ident_zero = sem("ident_zero")
        ident_ready = sem("ident_ready")
        topall_ready = sem("topall_ready")
        wext_ready = sem("wext_ready")
        pe_pro = sem("pe_pro")
        act_pro = sem("act_pro")
        dve_pro = sem("dve_pro")
        chain = sem("chain")
        vz_ready = sem("vz_ready")
        uw_ready = sem("uw_ready")
        exp_ready = sem("exp_ready")
        part_ready = sem("part_ready")
        first_ready = sem("first_ready")
        rest_ready = sem("rest_ready")
        second_ready = sem("second_ready")
        masked = sem("masked")
        turned = sem("turned")
        act_steps = sem("act_steps")
        dve_steps = sem("dve_steps")
        b_ready = sem("b_ready")
        b_used = sem("b_used")
        acc_done = sem("acc_done")
        act_evac = sem("act_evac")
        dve_evac = sem("dve_evac")
        g_chain = sem("g_chain")
        den_ready = sem("den_ready")
        rden_ready = sem("rden_ready")
        combined = sem("combined")
        neg_ready = sem("neg_ready")
        elu_exp = sem("elu_exp")
        cent_ready = sem("cent_ready")
        sq_ready = sem("sq_ready")
        var_ready = sem("var_ready")
        std_ready = sem("std_ready")
        y_ready = sem("y_ready")
        y_first = sem("y_first")
        y_second = sem("y_second")
        x2_top = sem("x2_top")
        x2_topall = sem("x2_topall")
        x2_scale = sem("x2_scale")
        x2_first = sem("x2_first")
        x2_second = sem("x2_second")
        gin_done = sem("gin_done")
        hid_ready = sem("hid_ready")
        mlp_done = sem("mlp_done")
        merged = sem("merged")
        sum_ready = sem("sum_ready")
        o_sq = sem("o_sq")
        o_var = sem("o_var")
        o_std = sem("o_std")
        o_ready = sem("o_ready")
        passed = sem("passed")

        def wait(eng, s, value):
            if not isinstance(value, int) or value > 0:
                eng.wait_ge(s, value)

        def wait_apart(eng, counts):
            for q, v in counts:
                wait(eng, q, v)
            eng.sem_inc(passed, 1)

        def attention_chunks(eng, chunk):
            chunk(0, 0)
            chunk(1, 1)
            with eng.Fori(0, (NC - 2) // 2) as i:
                chunk(i * 2 + 2, 0)
                chunk(i * 2 + 3, 1)

        steps = [(k, h) for k in range(K) for h in range(H)]
        act_share, dve_share = steps[:ACT_STEPS], steps[ACT_STEPS:]

        block = ctx.enter_context(nc.Block())

        @block.sync
        def _(sp):
            sp.dma_start(wext[:, 0:F], w).then_inc(w_landed, 16)
            sp.dma_start(a_all, a.partition_broadcast(P)).then_inc(w_landed, 16)
            for b in range(NB):
                sp.dma_start(xs[b * Q:(b + 1) * Q, :, :].rearrange("p (c k) f -> p c (k f)", k=K),
                             x_v[b]).then_inc(x_landed, 16)

            def load_chunk(n, c):
                for t in range(K):
                    wait(sp, masked, n * K + t - 1)
                    for b in (0, 2, 1, 3):
                        sp.dma_start(rows[b * Q:(b + 1) * Q, t % 2, :, :],
                                     adj_v[c, t, b]).then_inc(adj_landed[t % 2], 16)

            for l in range(L):
                sp.dma_start(wraw[:, l, :], w1[l]).then_inc(gin_w_landed, 16)
                sp.dma_start(wraw[:, L + l, :], w2[l]).then_inc(gin_w_landed, 16)
            sp.dma_start(wraw[:, 2 * L:2 * L + 2, :],
                         wm.rearrange("o (q i) -> o q i", q=2)).then_inc(gin_w_landed, 16)
            with nc.allow_non_contiguous_dma("a bias per partition"):
                sp.dma_start(bias[:, 0:L], b1.rearrange("l f -> f l")).then_inc(gin_w_landed, 16)
                sp.dma_start(bias[:, L:2 * L], b2.rearrange("l f -> f l")).then_inc(gin_w_landed, 16)
            sp.dma_start(bm_all[:], bm.partition_broadcast(P)).then_inc(gin_w_landed, 16)
            sp.dma_start(eps_all[:, 0:1], eps1.partition_broadcast(P)).then_inc(gin_w_landed, 16)
            sp.dma_start(eps_all[:, 1:2], eps2.partition_broadcast(P)).then_inc(gin_w_landed, 16)
            load_chunk(0, 0)
            with sp.Fori(1, NC) as n:
                load_chunk(n, n)
            with sp.Fori(0, NC) as n:
                load_chunk(n + NC, n)

        @block.gpsimd
        def _(pool):
            pool.memset(ident[:], 0.0).then_inc(ident_zero, 1)
            pool.wait_ge(ident_zero, 1)
            pool.affine_select(out=ident[:], in_=ident[:], compare_op=ALU.not_equal, fill=1.0, base=0,
                               pattern=[[-1, P]], channel_multiplier=1).then_inc(ident_ready, 1)
            pool.wait_ge(dve_pro, NC + NC)
            pool.dma_start(s_dram, s_rows).then_inc(s_stored, 16)
            pool.wait_ge(dve_pro, NC + NC + 1)
            pool.partition_all_reduce(topall[:], top[:], P, RMAX).then_inc(topall_ready, 1)
            pool.wait_ge(s_stored, 16)
            for n in range(2):
                pool.dma_start(s_all[:, n, :, :], s_v[n].partition_broadcast(P)).then_inc(s_landed[n], 16)

            def load_s(n, par):
                pool.wait_ge(act_steps, (n - 1) * NC)
                pool.wait_ge(dve_steps, (n - 1) * NC)
                pool.dma_start(s_all[:, par, :, :],
                               s_v[n].partition_broadcast(P)).then_inc(s_landed[par], 16)

            def combine(n, last=False):
                o = sums[:].rearrange("p t n -> p t n")
                full = o[:, :, 0:H * HB].rearrange("p t (h q g) -> p t h q g", h=H, q=4)
                az = o[:, :, H * HB:ACC].rearrange("p t (h q g) -> p t h q g", h=H, q=2)
                base = n * 4
                pool.wait_ge(act_evac, n * K + K)
                pool.wait_ge(dve_evac, n * K + K)
                for t in range(K):
                    last = pool.tensor_tensor(full[:, t, :, 2:4, :], az[:, t, :, :, :],
                                              full[:, t, :, 2:4, :], ALU.subtract)
                last.then_inc(g_chain, 1)
                wait_apart(pool, [(g_chain, base + 1)])
                for t in range(K):
                    last = pool.tensor_scalar(full[:, t, :, 1:4:2, :], full[:, t, :, 1:4:2, :],
                                              1.0 / SPLIT, None, ALU.mult)
                last.then_inc(g_chain, 1)
                pool.wait_ge(g_chain, base + 2)
                for t in range(K):
                    last = pool.tensor_tensor(full[:, t, :, 0:4:2, :], full[:, t, :, 0:4:2, :],
                                              full[:, t, :, 1:4:2, :], ALU.add)
                last.then_inc(g_chain, 1)
                pool.wait_ge(g_chain, base + 3)
                for q in range(2):
                    last = pool.tensor_tensor(
                        full[:, :, :, 2 * q, :], full[:, :, :, 2 * q, :],
                        uw[:, q, bass.ds(n * K, K), :].unsqueeze(3).to_broadcast([P, K, H, G]), ALU.mult)
                last.then_inc(g_chain, 1)
                pool.wait_ge(g_chain, base + 4)
                pool.tensor_tensor(full[:, :, :, 0, :], full[:, :, :, 0, :], full[:, :, :, 2, :],
                                   ALU.add).then_inc(den_ready, 1)
                pool.wait_ge(den_ready, n + 1)
                pool.wait_ge(rden_ready, n + 1)
                pool.tensor_tensor(
                    gat[:, bass.ds(n * K, K), :].rearrange("p t (h g) -> p t h g", h=H),
                    full[:, :, :, 0, 0:FH],
                    rden[:].unsqueeze(3).to_broadcast([P, K, H, FH]), ALU.mult).then_inc(combined, 1)

            pool.wait_ge(uw_ready, 2)
            combine(0)
            load_s(2, 0)
            combine(1)
            load_s(3, 1)
            with pool.Fori(0, (NC - 4) // 2) as i:
                combine(i * 2 + 2)
                load_s(i * 2 + 4, 0)
                combine(i * 2 + 3)
                load_s(i * 2 + 5, 1)
            combine(NC - 2)
            combine(NC - 1)
            pool.wait_ge(b_used, NC * NC)
            for b in range(NB):
                pool.dma_start(t_b[b * Q:(b + 1) * Q, :, :].rearrange("p (c k) f -> p c (k f)", k=K),
                               x2_v[b]).then_inc(x2_landed, 16)
            pool.wait_ge(x2_top, 1)
            pool.partition_all_reduce(x2top[:, 1:2], x2top[:, 0:1], P, RMAX).then_inc(x2_topall, 1)
            with pool.Fori(0, NC) as n:
                pool.wait_ge(o_ready, n + 1)
                for b in range(NB):
                    pool.dma_start(out_v[n, b],
                                   res[b * Q:(b + 1) * Q, 2, :, :].rearrange("p k f -> p (k f)")
                                   ).then_inc(out_stored, 16)
                pool.wait_ge(out_stored, (n + 1) * 16 * NB)

        @block.tensor
        def _(pe):
            pe.wait_ge(ident_ready, 1)
            pe.wait_ge(x_landed, 16 * NB)
            for g in range(NC):
                for k in range(K):
                    last = pe.transpose(ps[:, g, k * P:(k + 1) * P], xs[:, g * K + k, :], ident[:])
                last.then_inc(pe_pro, 1)
            pe.wait_ge(wext_ready, 1)
            for g in range(NC):
                pe.wait_ge(act_pro, g + 1)
                if g >= 4:
                    pe.wait_ge(act_pro, NC + g - 4 + 1)
                    pe.wait_ge(dve_pro, g - 4 + 1)
                if g == 0:
                    pe.wait_ge(act_pro, NC)
                for half in range(2):
                    bank = 2 * (g % 4) + half
                    for k in range(2):
                        t = g * K + 2 * half + k
                        last = pe.matmul(ps[:, bank, k * 256:k * 256 + F + 2 * H], xT[:, t * P:(t + 1) * P],
                                         wext[:], start=(k == 0), stop=(k == 1), skip_group_check=True)
                last.then_inc(pe_pro, 1)
            pe.wait_ge(act_pro, 2 * NC)
            pe.wait_ge(dve_pro, NC)
            for g in range(NC):
                pe.matmul(ps[0:H, g, :], wext[:, F + H:F + 2 * H], xT[:, g * CH:(g + 1) * CH],
                          start=True, stop=True).then_inc(pe_pro, 1)
            pe.wait_ge(gin_w_landed, 16 * (2 * L + 6))
            pe.wait_ge(dve_pro, 2 * NC)
            for j in range(2 * L + 2):
                last = pe.transpose(ps[:, j // 4, (j % 4) * P:(j % 4 + 1) * P], wraw[:, j, :], ident[:])
            last.then_inc(pe_pro, 1)
            pe.wait_ge(second_ready, 2 * H)
            pe.wait_ge(act_pro, 2 * NC + 1)

            def attend(n, par):
                for c in range(NC):
                    m = n * NC + c
                    wait_apart(pe, [(b_ready, m + 1)])
                    for t in range(K):
                        if c == 0:
                            wait_apart(pe, [(act_evac, n * K + (t + 1 - K)),
                                            (dve_evac, n * K + (t + 1 - K))])
                        for k in range(K):
                            cols = slice(t * P, (t + 1) * P)
                            for h in range(H):
                                bank, at = (2 * t, h * HB) if h < 3 else (2 * t + 1, 0)
                                mm = pe.matmul(ps[:, bank, at:at + HB], ringf8[:, c % RING, h, cols, k],
                                               hv[:, c * K + k, h, :],
                                               start=(c == 0 and k == 0 and h in (0, 3)),
                                               stop=(c == NC - 1 and k == K - 1), skip_group_check=True)
                            if t == K - 1 and k == K - 1:
                                mm.then_inc(b_used, 1)
                            mm = pe.matmul(ps[:, 2 * t + 1, HB:HB + H * 2 * G], maskTf8[:, par, c, cols, k],
                                           hv[:, c * K + k, :, 2 * G:4 * G],
                                           start=False, stop=(c == NC - 1 and k == K - 1),
                                           skip_group_check=True)
                        if c == NC - 1:
                            mm.then_inc(acc_done, 1)

            attention_chunks(pe, attend)

            def layers(n):
                def layer(l):
                    for q in range(2):
                        pe.wait_ge(hid_ready, n * (2 * L + 2) + 2 * l + q + 1)
                        pe.matmul(ps[:, 4 + q, :], wt[:, q * L + l, :], hid[:, 2 * q + l % 2, :],
                                  start=True, stop=True).then_inc(mlp_done, 1)

                def merge():
                    pe.wait_ge(hid_ready, n * (2 * L + 2) + 2 * L + 2)
                    wait(pe, sum_ready, n)
                    for k in range(K):
                        for q in range(2):
                            mm = pe.matmul(ps[:, 6, k * F:(k + 1) * F],
                                           hid[:, 2 * q + L % 2, k * P:(k + 1) * P], wt[:, 2 * L + q, :],
                                           start=(k == 0 and q == 0), stop=(q == 1), skip_group_check=True)
                    mm.then_inc(merged, 1)
                return [lambda l=l: layer(l) for l in range(L)] + [merge]

            def gather(n, par, before):
                work = layers(before) if before is not None else []
                wait_apart(pe, [(turned, n * K + (NC * K + K))])
                for c in range(NC):
                    if c == 0:
                        wait_apart(pe, [(hid_ready, n * (2 * L + 2) + (2 - 2 * (2 * L + 2)))])
                    for k in range(K):
                        for q in range(4):
                            mm = pe.matmul(ps[:, 2 * par + q // 2, :], yx[:, q, c * K + k, :],
                                           maskTf8[:, par, c, :, k],
                                           start=(c == 0 and k == 0 and q % 2 == 0),
                                           stop=(c == NC - 1 and k == K - 1 and q % 2 == 1))
                    if c == NC - 1:
                        mm.then_inc(gin_done, 1)
                    if work and c % 2 == 1:
                        work.pop(0)()

            pe.wait_ge(y_second, 1)
            pe.wait_ge(x2_second, 1)
            pe.wait_ge(act_evac, NC * K)
            pe.wait_ge(dve_evac, NC * K)
            gather(0, 0, None)
            gather(1, 1, 0)
            with pe.Fori(0, (NC - 2) // 2) as i:
                gather(i * 2 + 2, 0, i * 2 + 1)
                gather(i * 2 + 3, 1, i * 2 + 2)
            for step in layers(NC - 1):
                step()

        @block.scalar
        def _(act):
            for g in range(NC):
                act.wait_ge(pe_pro, g + 1)
                act.activation(xT[:, g * CH:(g + 1) * CH], ps[:, g, :], ACT.Copy).then_inc(act_pro, 1)
            for g in range(NC):
                act.wait_ge(pe_pro, NC + g + 1)
                for half in range(2):
                    t = g * K + 2 * half
                    last = act.activation(
                        gat[:, t:t + 2, :],
                        ps[:, 2 * (g % 4) + half, :].rearrange("p (k n) -> p k n", k=2)[:, :, 0:F], ACT.Copy)
                last.then_inc(act_pro, 1)
            act.wait_ge(exp_ready, 1)
            act.activation(vz[:, 0], ds[:, :, 0:H], ACT.Exp).then_inc(vz_ready, 1)
            act.activation(vz[:, 1], ds[:, :, 0:H], ACT.Exp, scale=SLOPE).then_inc(vz_ready, 1)
            act.wait_ge(exp_ready, 3)
            act.activation(uw[:, 0], uw[:, 0], ACT.Exp).then_inc(uw_ready, 1)
            act.activation(uw[:, 1], uw[:, 1], ACT.Exp, scale=-1.0).then_inc(uw_ready, 1)
            for j in range(2 * H):
                h, q = j // 2, j % 2
                act.wait_ge(part_ready, j + 1)
                act.activation(hv[:, :, h, 2 * q * G:(2 * q + 1) * G], part[:, j % 2],
                               ACT.Copy).then_inc(first_ready, 1)
                act.wait_ge(rest_ready, j + 1)
                act.activation(hv[:, :, h, (2 * q + 1) * G:(2 * q + 2) * G], part[:, j % 2],
                               ACT.Copy, scale=SPLIT).then_inc(second_ready, 1)
            act.wait_ge(pe_pro, 3 * NC + 1)
            act.activation(wt[:].rearrange("p l n -> p (l n)"),
                           ps[:, 0:2, :].rearrange("p b n -> p (b n)"), ACT.Copy).then_inc(act_pro, 1)
            act.wait_ge(act_pro, 2 * NC + 1)

            def evacuate(n):
                wait(act, combined, n)
                for t in range(K):
                    act.wait_ge(acc_done, n * K + (t + 1))
                    act.activation(sums[:, t, 0:BANK0], ps[:, 2 * t, 0:BANK0],
                                   ACT.Copy).then_inc(act_evac, 1)

            def compare(n, par):
                for c in range(NC):
                    m = n * NC + c
                    counts = [(b_used, m + (1 - RING))]
                    if c == 0:
                        counts.append((s_landed[par], (n + (2 - par)) * 8))
                    wait_apart(act, counts)
                    for k, h in act_share:
                        last = act.activation(ringf8[:, c % RING, h, :, k], s_all[:, par, h, :],
                                              ACT.Sigmoid, bias=dbig[:, c * K + k, h:h + 1],
                                              scale=STEP_GAIN, saturate=False)
                    last.then_inc(act_steps, 1)
                    if c == 1 and not (isinstance(n, int) and n == 0):
                        evacuate(n - 1)

            attention_chunks(act, compare)
            evacuate(NC - 1)

            act.wait_ge(neg_ready, 1)
            act.activation(t_a, t_a, ACT.Exp).then_inc(elu_exp, 1)
            act.wait_ge(x2_scale, 1)
            act.activation(yx[:, 2], t_b, ACT.Copy, scale=x2top[:, 2:3]).then_inc(x2_first, 1)
            act.wait_ge(cent_ready, 1)
            act.activation(t_a, xs[:], ACT.Square).then_inc(sq_ready, 1)
            act.wait_ge(var_ready, 1)
            act.activation(std[:], var[:], ACT.Sqrt).then_inc(std_ready, 1)
            act.wait_ge(y_ready, 1)
            act.activation(yx[:, 0], xs[:], ACT.Copy, scale=Y_GAIN).then_inc(y_first, 1)

            def gin_layers(n, par):
                base = n * (2 * L + 2)
                act.wait_ge(gin_done, n + 1)
                for q in range(2):
                    wait(act, merged, n)
                    act.activation(hid[:, 2 * q, :], ps[:, 2 * par + q, :], ACT.Copy,
                                   scale=gain[:, q:q + 1]).then_inc(hid_ready, 1)
                for l in range(L):
                    for q in range(2):
                        act.wait_ge(mlp_done, n * 2 * L + 2 * l + q + 1)
                        act.activation(hid[:, 2 * q + (l + 1) % 2, :], ps[:, 4 + q, :], ACT.Relu,
                                       bias=bias[:, q * L + l:q * L + l + 1]).then_inc(hid_ready, 1)
                act.wait_ge(o_var, n + 1)
                act.activation(std[:, 0:K], var[:, 0:K], ACT.Sqrt).then_inc(o_std, 1)

            gin_layers(0, 0)
            gin_layers(1, 1)
            with act.Fori(0, (NC - 2) // 2) as i:
                gin_layers(i * 2 + 2, 0)
                gin_layers(i * 2 + 3, 1)

        @block.vector
        def _(dve):
            links = [0]

            def link(ins):
                links[0] += 1
                ins.then_inc(chain, 1)
                dve.wait_ge(chain, links[0])

            dve.wait_ge(w_landed, 32)
            wv = wext[:, 0:F].rearrange("p (h f) -> p h f", h=H)
            for q, at in ((1, F), (0, F + H)):
                link(dve.tensor_tensor(part[:, 0, 0:H, 0:FH], wv, a_all[:, :, q * FH:(q + 1) * FH], ALU.mult))
                last = dve.tensor_reduce(wext[:, at:at + H], part[:, 0, 0:H, 0:FH], X, ALU.add)
                if q == 1:
                    link(last)
            last.then_inc(wext_ready, 1)
            for g in range(NC):
                dve.wait_ge(act_pro, NC + g + 1)
                for half in range(2):
                    t = g * K + 2 * half
                    last = dve.tensor_copy(
                        ds[:, t:t + 2, :],
                        ps[:, 2 * (g % 4) + half, :].rearrange("p (k n) -> p k n", k=2)[:, :, F:F + 2 * H])
                last.then_inc(dve_pro, 1)
            for g in range(NC):
                dve.wait_ge(pe_pro, 2 * NC + g + 1)
                dve.tensor_copy(s_rows[:, g * CH:(g + 1) * CH], ps[0:H, g, :]).then_inc(dve_pro, 1)
            dve.wait_ge(dve_pro, NC)
            dve.wait_ge(act_pro, 2 * NC)
            dve.tensor_reduce(top[:, 0:H], ds[:, :, 0:H].rearrange("p t h -> p h t"), X, ALU.max)
            dve.tensor_scalar(dneg[:], ds[:, :, 0:H], -1.0, None, ALU.mult)
            link(dve.tensor_scalar(dbig[:], ds[:, :, 0:H], STEP_GAIN, None, ALU.mult))
            dve.tensor_reduce(top[:, H:H + 1], gat[:].rearrange("p t f -> p (t f)"), X, ALU.max,
                              apply_absolute_value=True).then_inc(dve_pro, 1)
            dve.wait_ge(topall_ready, 1)
            dall = topall[:, 0:H].unsqueeze(1).to_broadcast([P, NT, H])
            link(dve.tensor_tensor(ds[:, :, H:2 * H], ds[:, :, H:2 * H], dall, ALU.add))
            dve.tensor_tensor(ds[:, :, 0:H], ds[:, :, 0:H], dall, ALU.subtract).then_inc(exp_ready, 1)
            dve.tensor_scalar(uw[:, 0], ds[:, :, H:2 * H], 1.0 - SLOPE, 0.0, ALU.mult,
                              ALU.min).then_inc(exp_ready, 1)
            dve.tensor_scalar(uw[:, 1], ds[:, :, H:2 * H], 1.0 - SLOPE, 0.0, ALU.mult,
                              ALU.max).then_inc(exp_ready, 1)
            link(dve.tensor_scalar(topall[:, H:H + 1], topall[:, H:H + 1], 1e-30, None, ALU.max))
            link(dve.reciprocal(hscale[:], topall[:, H:H + 1]))
            link(dve.tensor_scalar(gat[:], gat[:], hscale[:, 0:1], None, ALU.mult))
            dve.wait_ge(vz_ready, 2)
            link(dve.tensor_scalar(vz.rearrange("p q t h -> p (q t h)"),
                                   vz.rearrange("p q t h -> p (q t h)"), HP_TOP, None, ALU.mult))
            for j in range(2 * H):
                h, q = j // 2, j % 2
                wait(dve, second_ready, j - 1)
                dve.tensor_copy(part[:, j % 2, :, FH], vz[:, q, :, h])
                dve.tensor_tensor(part[:, j % 2, :, 0:FH], gat[:, :, h * FH:(h + 1) * FH],
                                  vz[:, q, :, h:h + 1].to_broadcast([P, NT, FH]),
                                  ALU.mult).then_inc(part_ready, 1)
                dve.wait_ge(part_ready, j + 1)
                dve.wait_ge(first_ready, j + 1)
                dve.tensor_tensor(part[:, j % 2], part[:, j % 2], hv[:, :, h, 2 * q * G:(2 * q + 1) * G],
                                  ALU.subtract).then_inc(rest_ready, 1)

            def turn(n, par, t):
                s = n * K + t
                dve.wait_ge(adj_landed[t % 2], (n * 2 + (t // 2 + 1)) * 16 * NB)
                wait(dve, turned, s - 1)
                dve.tensor_scalar(mask[:, t % 2, :], rows[:, t % 2, :, :].rearrange("p b j -> p (b j)"),
                                  0.0, FP8_ONE, ALU.is_gt, ALU.mult).then_inc(masked, 1)
                dve.wait_ge(masked, s + 1)
                dve.transpose(
                    maskT[:, par, :, t * P:(t + 1) * P].rearrange("p c (b i) -> p b c i", b=NB),
                    mask[:, t % 2, :].bitcast(I32).rearrange("p (b c w) -> p b c w", b=NB, w=Q)
                ).then_inc(turned, 1)

            for t in range(K):
                turn(0, 0, t)

            def evacuate(n):
                wait(dve, combined, n)
                for t in range(K):
                    dve.wait_ge(acc_done, n * K + (t + 1))
                    dve.tensor_copy(sums[:, t, BANK0:ACC], ps[:, 2 * t + 1, 0:ACC - BANK0]).then_inc(dve_evac, 1)

            def reciprocals(n):
                dve.wait_ge(den_ready, n + 1)
                dve.reciprocal(rden[:], sums[:, :, 0:H * HB].rearrange("p t (h n) -> p t h n", h=H)[:, :, :, FH]
                               ).then_inc(rden_ready, 1)

            def mask_group(n, par, c):
                m = n * NC + c
                dve.wait_ge(act_steps, m + 1)
                dve.wait_ge(dve_steps, m + 1)
                dve.tensor_tensor(ring[:, c % RING], ring[:, c % RING],
                                  maskT[:, par, c:c + 1, :].to_broadcast([P, H, CH]),
                                  ALU.bitwise_and).then_inc(b_ready, 1)

            def compare(n, par):
                first = isinstance(n, int) and n == 0
                for c in range(NC):
                    m = n * NC + c
                    wait(dve, b_used, m + (1 - RING))
                    if c == 0:
                        dve.wait_ge(s_landed[par], (n + (2 - par)) * 8)
                        dve.wait_ge(turned, n * K + K)
                    for k, h in dve_share:
                        last = dve.tensor_scalar(ring8[:, c % RING, h, :, k], s_all[:, par, h, :],
                                                 dneg[:, c * K + k, h:h + 1], FP8_ONE, ALU.is_gt, ALU.mult)
                    last.then_inc(dve_steps, 1)
                    if c > 0:
                        mask_group(n, par, c - 1)
                    if c == 1 and not first:
                        evacuate(n - 1)
                    if c == 4 and not first:
                        reciprocals(n - 1)
                    if c % 2 == 1:
                        if c == 1:
                            wait(dve, acc_done, n * K)
                        turn(n + 1, 1 - par, c // 2)
                mask_group(n, par, NC - 1)

            dve.wait_ge(act_pro, 2 * NC + 1)
            attention_chunks(dve, compare)
            evacuate(NC - 1)
            reciprocals(NC - 1)

            am = topall[:, H:H + 1]
            dve.wait_ge(combined, NC)
            dve.wait_ge(b_used, NC * NC)
            dve.tensor_scalar(t_a, gat[:], am, 0.0, ALU.mult, ALU.min).then_inc(neg_ready, 1)
            link(dve.tensor_scalar(gat[:], gat[:], am, 0.0, ALU.mult, ALU.max))
            link(dve.tensor_tensor(xs[:], xs[:], gat[:], ALU.add))
            dve.wait_ge(x2_landed, 16 * NB)
            dve.tensor_reduce(x2top[:, 0:1], t_b.rearrange("p t f -> p (t f)"), X, ALU.max,
                              apply_absolute_value=True).then_inc(x2_top, 1)
            dve.wait_ge(elu_exp, 1)
            link(dve.scalar_tensor_tensor(out=xs[:], in0=t_a, scalar=-1.0, in1=xs[:],
                                          op0=ALU.add, op1=ALU.add))
            dve.wait_ge(x2_topall, 1)
            link(dve.tensor_scalar(x2top[:, 1:2], x2top[:, 1:2], 1e-30, None, ALU.max))
            link(dve.tensor_scalar(x2top[:, 3:4], x2top[:, 1:2], 1.0 / HP_TOP, None, ALU.mult))
            dve.reciprocal(x2top[:, 2:3], x2top[:, 3:4]).then_inc(x2_scale, 1)
            link(dve.tensor_reduce(mean[:], xs[:], X, ALU.add))
            link(dve.tensor_scalar(mean[:], mean[:], 1.0 / F, None, ALU.mult))
            dve.tensor_tensor(xs[:], xs[:], mean[:].unsqueeze(2).to_broadcast([P, NT, F]),
                              ALU.subtract).then_inc(cent_ready, 1)
            dve.wait_ge(x2_first, 1)
            dve.scalar_tensor_tensor(out=yx[:, 3], in0=t_b, scalar=x2top[:, 2:3], in1=yx[:, 2],
                                     op0=ALU.mult, op1=ALU.subtract).then_inc(x2_second, 1)
            dve.wait_ge(sq_ready, 1)
            link(dve.tensor_reduce(var[:], t_a, X, ALU.add))
            dve.tensor_scalar(var[:], var[:], 1.0 / F, LN_EPS, ALU.mult, ALU.add).then_inc(var_ready, 1)
            dve.wait_ge(std_ready, 1)
            link(dve.reciprocal(rstd[:], std[:]))
            dve.tensor_tensor(xs[:], xs[:], rstd[:].unsqueeze(2).to_broadcast([P, NT, F]),
                              ALU.mult).then_inc(y_ready, 1)
            dve.wait_ge(gin_w_landed, 16 * (2 * L + 6))
            dve.tensor_scalar(gain[:, 0:1], eps_all[:, 0:1], 2.0, 1.0 / Y_GAIN, ALU.add, ALU.mult)
            dve.tensor_scalar(gain[:, 1:2], eps_all[:, 1:2], 2.0, x2top[:, 3:4], ALU.add, ALU.mult)
            dve.wait_ge(y_ready, 1)
            dve.wait_ge(y_first, 1)
            dve.scalar_tensor_tensor(out=yx[:, 1], in0=xs[:], scalar=Y_GAIN, in1=yx[:, 0],
                                     op0=ALU.mult, op1=ALU.subtract).then_inc(y_second, 1)
            link(dve.tensor_tensor(xs[:], xs[:], bm_all[:].unsqueeze(1).to_broadcast([P, NT, F]), ALU.add))

            def finish(n):
                cen, sq, o = res[:, 0], res[:, 1], res[:, 2]
                at = n * 5
                base = links[0]
                wait(dve, o_ready, n)
                dve.wait_ge(merged, n + 1)
                dve.tensor_tensor(cen, ps[:, 6, :].rearrange("p (k f) -> p k f", k=K),
                                  xs[:, bass.ds(n * K, K), :], ALU.add).then_inc(sum_ready, 1)
                dve.wait_ge(sum_ready, n + 1)
                dve.tensor_reduce(mean[:, 0:K], cen, X, ALU.add).then_inc(chain, 1)
                dve.wait_ge(chain, at + (base + 1))
                dve.tensor_scalar(mean[:, 0:K], mean[:, 0:K], 1.0 / F, None, ALU.mult).then_inc(chain, 1)
                dve.wait_ge(chain, at + (base + 2))
                dve.tensor_tensor(cen, cen, mean[:, 0:K].unsqueeze(2).to_broadcast([P, K, F]),
                                  ALU.subtract).then_inc(chain, 1)
                dve.wait_ge(chain, at + (base + 3))
                dve.tensor_tensor(sq, cen, cen, ALU.mult).then_inc(chain, 1)
                dve.wait_ge(chain, at + (base + 4))
                dve.tensor_reduce(var[:, 0:K], sq, X, ALU.add).then_inc(o_sq, 1)
                dve.wait_ge(o_sq, n + 1)
                dve.tensor_scalar(var[:, 0:K], var[:, 0:K], 1.0 / F, LN_EPS, ALU.mult,
                                  ALU.add).then_inc(o_var, 1)
                dve.wait_ge(o_std, n + 1)
                dve.reciprocal(rstd[:, 0:K], std[:, 0:K]).then_inc(chain, 1)
                dve.wait_ge(chain, at + (base + 5))
                wait(dve, out_stored, n * (16 * NB))
                dve.tensor_tensor(o, cen, rstd[:, 0:K].unsqueeze(2).to_broadcast([P, K, F]),
                                  ALU.mult).then_inc(o_ready, 1)

            def gin_chunk(n, par):
                wait(dve, gin_done, n)
                if not (isinstance(n, int) and n == NC - 1):
                    for t in range(K):
                        turn(n + (NC + 1), 1 - par, t)
                if not (isinstance(n, int) and n == 0):
                    finish(n - 1)

            gin_chunk(0, 0)
            gin_chunk(1, 1)
            with dve.Fori(0, (NC - 4) // 2) as i:
                gin_chunk(i * 2 + 2, 0)
                gin_chunk(i * 2 + 3, 1)
            gin_chunk(NC - 2, 0)
            gin_chunk(NC - 1, 1)
            finish(NC - 1)


_INS = ['x', 'adj', 'L0_gnn_W', 'L0_gnn_a', 'L1_gnn_x2', 'L1_gnn_eps1', 'L1_gnn_eps2', 'L1_gnn_W1',
        'L1_gnn_b1', 'L1_gnn_W2', 'L1_gnn_b2', 'L1_gnn_Wm', 'L1_gnn_bm']
_OUTS = [((4096, 128), 'float32')]


def kernel(**inputs):
    import numpy as _np
    import concourse.bacc as _bacc
    from concourse import mybir as _mybir
    from concourse.bass_utils import run_bass_kernel_spmd as _run

    nc = _bacc.Bacc("TRN2", target_bir_lowering=False, num_devices=1)
    arrays, args = {}, []
    for name in _INS:
        a = _np.ascontiguousarray(inputs[name])
        arrays[f"in_{name}_dram"] = a
        args.append(nc.dram_tensor(f"in_{name}_dram", a.shape, _mybir.dt.from_np(a.dtype), kind="ExternalInput").ap())
    for i, (shape, dtype) in enumerate(_OUTS):
        dt = _mybir.dt.from_np(_np.dtype(dtype))
        args.append(nc.dram_tensor(f"out_{i}_dram", shape, dt, kind="ExternalOutput").ap())
    gat_gin_resnorm_kernel(nc, *args)
    r = _run(nc, [arrays], core_ids=[0])
    got = tuple(r.results[0][f"out_{i}_dram"] for i in range(len(_OUTS)))
    return got[0]
```

```python
from contextlib import ExitStack

import concourse.bass as bass
from concourse import mybir

F32 = mybir.dt.float32
F16 = mybir.dt.float16
F8 = mybir.dt.float8e4
U8 = mybir.dt.uint8
I32 = mybir.dt.int32
ALU = mybir.AluOpType
ACT = mybir.ActivationFunctionType
X = mybir.AxisListType.X
RMAX = bass.bass_isa.ReduceOp.max

P = 128
Q = 32
NB = P // Q
K = 4
MASK_BYTE = 64.0
MASK_ONE = 2.0
STEP_GAIN = 2.0 ** 60
SPLIT = 2.0 ** 11
HP_TOP = 2.0 ** 13
Y_GAIN = 2.0 ** 10
RING = 4
PARTS = 4
ACT_STEPS = 10
SLOPE = 0.2
LN_EPS = 1e-5


def gat_gin_resnorm_kernel(nc, x, adj, w, a, x2, eps1, eps2, w1, b1, w2, b2, wm, bm, out):
    N, F = x.shape
    H, FH = a.shape[0], a.shape[1] // 2
    NT = N // P
    NC = NT // K
    CH = K * P
    JB = N // NB
    G = FH + 1
    HB = 4 * G
    ACC = H * HB + H * 2 * G
    BANK0 = 3 * HB
    L = w1.shape[0]

    with ExitStack() as ctx:
        def sb(name, shape, dt):
            return ctx.enter_context(nc.sbuf_tensor(name, shape, dt))

        def sem(name):
            return ctx.enter_context(nc.semaphore(name))

        KEPT = 2
        s_dram = nc.dram_tensor("s_rows", [H, N], F32).ap()
        mask_dram = nc.dram_tensor("mask_words", [NC - KEPT, P, NC * CH], I32).ap()

        xs = sb("xs", [P, NT, F], F32)
        gat = sb("gat", [P, NT, F], F32)
        hv = sb("hv", [P, NT, H, HB], F16)
        rows = sb("rows", [P, 2, NB, JB], F32)
        mask = sb("mask", [P, 2, NB * JB], U8)
        maskT = sb("maskT", [P, 2, NC, CH], I32)
        ring = sb("ring", [P, RING, H, CH], I32)
        s_all = sb("s_all", [P, 2, H, CH], F32)
        sums = sb("sums", [P, K, ACC], F32)
        ident = sb("ident", [P, P], F32)
        wext = sb("wext", [P, F + 2 * H], F32)
        ds = sb("ds", [P, NT, 2 * H], F32)
        dneg = sb("dneg", [P, NT, H], F32)
        dbig = sb("dbig", [P, NT, H], F32)
        uw = sb("uw", [P, 2, NT, H], F32)
        top = sb("top", [P, H + 1], F32)
        topall = sb("topall", [P, H + 1], F32)
        top_xw = sb("top_xw", [P, NC], F32)
        hscale = sb("hscale", [P, 1], F32)
        rden = sb("rden", [P, K, H], F32)
        x2top = sb("x2top", [P, 5], F32)
        wt = sb("wt", [P, 2 * L + 2, P], F32)
        bias = sb("bias", [P, 2 * L], F32)
        bm_all = sb("bm_all", [P, F], F32)
        gain = sb("gain", [P, 2], F32)
        eps_all = sb("eps_all", [P, 2], F32)
        stats = sb("stats", [P, NT, 6], F32)
        moments = sb("moments", [P, K, 2], F32)
        mean = sb("mean", [P, NT], F32)
        spread = sb("spread", [P, NT], F32)
        var = sb("var", [P, NT], F32)
        std = sb("std", [P, NT], F32)
        ln_eps = sb("ln_eps", [P, 1], F32)
        rstd = sb("rstd", [P, NT], F32)
        ps = ctx.enter_context(nc.psum_tensor("ps", [P, 8, 512], F32))

        flat_ring = ring[:].rearrange("p r h i -> p (r h i)").bitcast(F32)
        xT = flat_ring[:, 0:N]
        wraw = flat_ring[:, RING * H * CH - (2 * L + 2) * P:].rearrange("p (l n) -> p l n", n=P)
        part = flat_ring[:, 0:PARTS * NT * G].rearrange("p (r t g) -> p r t g", r=PARTS, g=G)
        s_rows = s_all[:].rearrange("p r h i -> p (r h i)")[0:H, :]
        flat_sums = sums[:].rearrange("p t n -> p (t n)")
        w_a = flat_sums[:, 0:F].rearrange("p (h f) -> p h f", h=H)
        a_all = flat_sums[:, F:F + H * 2 * FH].rearrange("p (h f) -> p h f", h=H)
        vz = flat_sums[:, ACC * K - 2 * NT * H:ACC * K].rearrange("p (q t h) -> p q t h", q=2, h=H)
        vz_den = flat_sums[:, ACC * K - 4 * NT * H:ACC * K - 2 * NT * H].rearrange(
            "p (q t h) -> p q t h", q=2, h=H)
        x2raw = rows[:, 0].rearrange("p b j -> p (b j)").rearrange("p (t f) -> p t f", f=F)
        x2part = rows[:, 1].rearrange("p b j -> p (b j)").bitcast(F16).rearrange(
            "p (q t f) -> p q t f", q=2, f=F)
        ypart = gat[:].rearrange("p t f -> p (t f)").bitcast(F16).rearrange(
            "p (c q k f) -> p c q k f", q=2, k=K, f=F)
        hid = s_all[:].rearrange("p r h i -> p (r h) i")
        res = flat_sums[:, 0:3 * K * F].rearrange("p (r k f) -> p r k f", r=3, f=F)

        ring8 = ring[:].rearrange("p r h i -> p (r h i)").bitcast(U8).rearrange(
            "p (r h i k) -> p r h i k", r=RING, h=H, k=K)
        ringf8 = ring[:].rearrange("p r h i -> p (r h i)").bitcast(F8).rearrange(
            "p (r h i k) -> p r h i k", r=RING, h=H, k=K)
        maskTf8 = maskT[:].rearrange("p r c i -> p (r c i)").bitcast(F8).rearrange(
            "p (r c i k) -> p r c i k", r=2, c=NC, k=K)

        x_v = x.rearrange("(b c w k) f -> b w c (k f)", b=NB, c=NC, w=Q)
        x2_v = x2.rearrange("(b c w k) f -> b w c (k f)", b=NB, c=NC, w=Q)
        out_v = out.rearrange("(b c w k) f -> c b w (k f)", b=NB, c=NC, w=Q)
        adj_v = adj.rearrange("(B c w k) (b j) -> c k b w B j", B=NB, c=NC, w=Q, b=NB)
        mask_v = [maskT[:, r].rearrange("p c i -> p (c i)") for r in range(2)]
        s_v = s_dram.rearrange("h (c i) -> c h i", i=CH)

        x_landed = sem("x_landed")
        w_landed = sem("w_landed")
        gin_w_landed = sem("gin_w_landed")
        x2_landed = sem("x2_landed")
        adj_landed = [sem(f"adj_landed{r}") for r in range(2)]
        s_stored = sem("s_stored")
        xw_top = sem("xw_top")
        s_landed = [sem(f"s_landed{r}") for r in range(2)]
        mask_stored = sem("mask_stored")
        mask_landed = [sem(f"mask_landed{r}") for r in range(2)]
        out_stored = sem("out_stored")
        ident_zero = sem("ident_zero")
        ident_ready = sem("ident_ready")
        topall_ready = sem("topall_ready")
        wext_ready = sem("wext_ready")
        pe_pro = sem("pe_pro")
        act_pro = sem("act_pro")
        dve_pro = sem("dve_pro")
        chain = sem("chain")
        vz_ready = sem("vz_ready")
        uw_ready = sem("uw_ready")
        exp_ready = sem("exp_ready")
        vz_scaled = sem("vz_scaled")
        pool_parts = sem("pool_parts")
        dve_parts = sem("dve_parts")
        den_cols = sem("den_cols")
        den_cols_rest = sem("den_cols_rest")
        first_ready = sem("first_ready")
        second_ready = sem("second_ready")
        masked = sem("masked")
        turned = sem("turned")
        act_steps = sem("act_steps")
        dve_steps = sem("dve_steps")
        b_ready = sem("b_ready")
        b_used = sem("b_used")
        acc_done = sem("acc_done")
        act_evac = sem("act_evac")
        dve_evac = sem("dve_evac")
        g_chain = sem("g_chain")
        den_ready = sem("den_ready")
        rden_ready = sem("rden_ready")
        combined = sem("combined")
        neg_ready = sem("neg_ready")
        neg_rest = sem("neg_rest")
        x_added = sem("x_added")
        den_scaled = sem("den_scaled")
        elu_exp = sem("elu_exp")
        var_ready = sem("var_ready")
        std_ready = sem("std_ready")
        y_ready = sem("y_ready")
        y_first = sem("y_first")
        y_second = sem("y_second")
        stats_ready = sem("stats_ready")
        x2_top = sem("x2_top")
        x2_topall = sem("x2_topall")
        x2_scale = sem("x2_scale")
        x2_first = sem("x2_first")
        x2_second = sem("x2_second")
        gin_done = sem("gin_done")
        hid_ready = sem("hid_ready")
        mlp_done = sem("mlp_done")
        merged = sem("merged")
        sum_ready = sem("sum_ready")
        half_sums = sem("half_sums")
        o_var = sem("o_var")
        o_std = sem("o_std")
        o_ready = sem("o_ready")
        passed = sem("passed")

        def wait(eng, s, value):
            if not isinstance(value, int) or value > 0:
                eng.wait_ge(s, value)

        def wait_apart(eng, counts):
            for q, v in counts:
                wait(eng, q, v)
            eng.sem_inc(passed, 1)

        def attention_chunks(eng, chunk):
            chunk(0, 0)
            chunk(1, 1)
            with eng.Fori(0, (NC - 4) // 2) as i:
                chunk(i * 2 + 2, 0)
                chunk(i * 2 + 3, 1)
            chunk(NC - 2, 0)
            chunk(NC - 1, 1)

        def gin_chunks(eng, step):
            for p in range(KEPT):
                step(p, NC - KEPT + p, p)
            with eng.Fori(0, (NC - KEPT) // 2) as i:
                step(i * 2 + 2, i * 2, 0)
                step(i * 2 + 3, i * 2 + 1, 1)

        full = sums[:, :, 0:H * HB].rearrange("p t (h q g) -> p t h q g", h=H, q=4)
        az = sums[:, :, H * HB:ACC].rearrange("p t (h q g) -> p t h q g", h=H, q=2)
        g_out = full[:, :, :, 1, 0:FH]
        neg = full[:, :, :, 2, 0:FH]

        def combine_sums(eng, n, tiles, settle):
            for t in tiles:
                last = eng.tensor_tensor(full[:, t, :, 2:4, :], az[:, t], full[:, t, :, 2:4, :],
                                         ALU.subtract)
            settle(last)
            for t in tiles:
                last = eng.tensor_scalar(full[:, t, :, 1:4:2, :], full[:, t, :, 1:4:2, :],
                                         1.0 / SPLIT, None, ALU.mult)
            settle(last)
            for t in tiles:
                last = eng.tensor_tensor(full[:, t, :, 0:4:2, :], full[:, t, :, 0:4:2, :],
                                         full[:, t, :, 1:4:2, :], ALU.add)
            settle(last)
            t0, t1 = tiles[0], tiles[-1] + 1
            for q in range(2):
                last = eng.tensor_tensor(
                    full[:, t0:t1, :, 2 * q, :], full[:, t0:t1, :, 2 * q, :],
                    uw[:, q, bass.ds(n * K + t0, t1 - t0), :].unsqueeze(3).to_broadcast(
                        [P, t1 - t0, H, G]), ALU.mult)
            settle(last)
            return eng.tensor_tensor(full[:, t0:t1, :, 0, :], full[:, t0:t1, :, 0, :],
                                     full[:, t0:t1, :, 2, :], ALU.add)

        def rows_of(buf, n, tiles):
            return buf[:, bass.ds(n * K + tiles[0], len(tiles)), :].rearrange("p t (h g) -> p t h g", h=H)

        def attention_output(eng, n, tiles):
            t0, t1 = tiles[0], tiles[-1] + 1
            return eng.tensor_tensor(g_out[:, t0:t1], full[:, t0:t1, :, 0, 0:FH],
                                     rden[:, t0:t1].unsqueeze(3).to_broadcast([P, t1 - t0, H, FH]), ALU.mult)

        steps = [(k, h) for k in range(K) for h in range(H)]
        act_share, dve_share = steps[:ACT_STEPS], steps[ACT_STEPS:]

        pool_tiles, dve_tiles = (0,), tuple(range(1, K))
        pool_share, mult_share = (0, 1, 2, 4, 5), (3, 6, 7)

        def operand(eng, j, cols, ready):
            h, q = j // 2, j % 2
            eng.tensor_copy(part[:, j % PARTS, :, FH], vz_den[:, q, :, h]).then_inc(cols, 1)
            eng.tensor_tensor(part[:, j % PARTS, :, 0:FH], gat[:, :, h * FH:(h + 1) * FH],
                              vz[:, q, :, h:h + 1].to_broadcast([P, NT, FH]), ALU.mult).then_inc(ready, 1)

        block = ctx.enter_context(nc.Block())

        @block.sync
        def _(sp):
            sp.dma_start(wext[:, 0:F], w).then_inc(w_landed, 16)
            sp.dma_start(a_all, a.partition_broadcast(P)).then_inc(w_landed, 16)
            for b in range(NB):
                sp.dma_start(xs[b * Q:(b + 1) * Q, :, :].rearrange("p (c k) f -> p c (k f)", k=K),
                             x_v[b]).then_inc(x_landed, 16)

            def load_chunk(n, c, store=False):
                for t in range(K):
                    if store and t == 2:
                        sp.wait_ge(turned, n * K)
                        sp.dma_start(mask_dram[n - 1], mask_v[store - 1]).then_inc(mask_stored, 16)
                    wait(sp, masked, n * K + t - 1)
                    for b in (0, 2, 1, 3):
                        sp.dma_start(rows[b * Q:(b + 1) * Q, t % 2, :, :],
                                     adj_v[c, t, b]).then_inc(adj_landed[t % 2], 16)

            for l in range(L):
                sp.dma_start(wraw[:, l, :], w1[l]).then_inc(gin_w_landed, 16)
                sp.dma_start(wraw[:, L + l, :], w2[l]).then_inc(gin_w_landed, 16)
            sp.dma_start(wraw[:, 2 * L:2 * L + 2, :],
                         wm.rearrange("o (q i) -> o q i", q=2)).then_inc(gin_w_landed, 16)
            with nc.allow_non_contiguous_dma("a bias per partition"):
                sp.dma_start(bias[:, 0:L], b1.rearrange("l f -> f l")).then_inc(gin_w_landed, 16)
                sp.dma_start(bias[:, L:2 * L], b2.rearrange("l f -> f l")).then_inc(gin_w_landed, 16)
            sp.dma_start(bm_all[:], bm.partition_broadcast(P)).then_inc(gin_w_landed, 16)
            sp.dma_start(eps_all[:, 0:1], eps1.partition_broadcast(P)).then_inc(gin_w_landed, 16)
            sp.dma_start(eps_all[:, 1:2], eps2.partition_broadcast(P)).then_inc(gin_w_landed, 16)
            load_chunk(0, 0)
            with sp.Fori(0, (NC - KEPT) // 2) as i:
                load_chunk(i * 2 + 1, i * 2 + 1, store=1)
                load_chunk(i * 2 + 2, i * 2 + 2, store=2)
            load_chunk(NC - 1, NC - 1)
            sp.wait_ge(masked, NC * K)
            for b in range(NB):
                sp.dma_start(x2raw[b * Q:(b + 1) * Q, :, :].rearrange("p (c k) f -> p c (k f)", k=K),
                             x2_v[b]).then_inc(x2_landed, 16)
            sp.wait_ge(mask_stored, 16 * (NC - KEPT))
            with sp.Fori(0, (NC - KEPT) // 2) as i:
                for r in range(2):
                    sp.wait_ge(gin_done, i * 2 + (r + 1))
                    sp.dma_start(mask_v[r], mask_dram[i * 2 + r]).then_inc(mask_landed[r], 16)

        @block.gpsimd
        def _(pool):
            pool.memset(ident[:], 0.0).then_inc(ident_zero, 1)
            pool.wait_ge(ident_zero, 1)
            pool.affine_select(out=ident[:], in_=ident[:], compare_op=ALU.not_equal, fill=1.0, base=0,
                               pattern=[[-1, P]], channel_multiplier=1).then_inc(ident_ready, 1)
            pool.wait_ge(dve_pro, NC + 1)
            pool.partition_all_reduce(topall[:], top[:], P, RMAX).then_inc(topall_ready, 1)
            pool.wait_ge(dve_pro, NC + 1 + NC // 2)
            pool.wait_ge(act_pro, 2 * NC + NC // 2)
            pool.dma_start(s_dram, s_rows).then_inc(s_stored, 16)
            pool.wait_ge(s_stored, 16)
            for n in range(2):
                pool.dma_start(s_all[:, n, :, :], s_v[n].partition_broadcast(P)).then_inc(s_landed[n], 16)
            pool.wait_ge(vz_scaled, 1)
            pool.wait_ge(pe_pro, 3 * NC)
            for at, j in enumerate(pool_share):
                wait(pool, second_ready, j + 1 - PARTS)
                operand(pool, j, den_cols, pool_parts)

            def load_s(n, par):
                pool.wait_ge(act_steps, (n - 1) * NC)
                pool.wait_ge(dve_steps, (n - 1) * NC)
                pool.dma_start(s_all[:, par, :, :],
                               s_v[n].partition_broadcast(P)).then_inc(s_landed[par], 16)

            def combine(n, tiles=tuple(range(K))):
                base = n * 6
                made = [0]

                def settle(ins):
                    ins.then_inc(g_chain, 1)
                    made[0] += 1
                    wait_apart(pool, [(g_chain, base + made[0])])

                pool.wait_ge(act_evac, n * K + K)
                pool.wait_ge(dve_evac, n * K + K)
                combine_sums(pool, n, tiles, settle).then_inc(den_ready, 1)
                pool.wait_ge(den_ready, n + 1)
                pool.wait_ge(rden_ready, n + 1)
                settle(attention_output(pool, n, tiles))
                t0, t1 = tiles[0], tiles[-1] + 1
                pool.tensor_scalar(neg[:, t0:t1], g_out[:, t0:t1], 0.0, None,
                                   ALU.min).then_inc(neg_ready, 1)
                settle(pool.tensor_scalar(g_out[:, t0:t1], g_out[:, t0:t1], 0.0, -1.0,
                                          ALU.max, ALU.add))
                pool.tensor_tensor(rows_of(xs, n, tiles), rows_of(xs, n, tiles), g_out[:, t0:t1],
                                   ALU.add).then_inc(x_added, 1)
                wait_apart(pool, [(x_added, n + 1), (elu_exp, n + 1)])
                pool.tensor_tensor(rows_of(xs, n, tiles), rows_of(xs, n, tiles), neg[:, t0:t1],
                                   ALU.add).then_inc(combined, 1)

            pool.wait_ge(uw_ready, 2)
            combine(0)
            load_s(2, 0)
            combine(1)
            load_s(3, 1)
            with pool.Fori(0, (NC - 4) // 2) as i:
                combine(i * 2 + 2)
                load_s(i * 2 + 4, 0)
                combine(i * 2 + 3)
                load_s(i * 2 + 5, 1)
            pool.wait_ge(x2_top, 1)
            pool.partition_all_reduce(x2top[:, 1:2], x2top[:, 0:1], P, RMAX).then_inc(x2_topall, 1)
            combine(NC - 2)
            combine(NC - 1, pool_tiles)

            def store(p, c, par):
                pool.wait_ge(o_ready, p + 1)
                for b in range(NB):
                    pool.dma_start(out_v[c, b],
                                   res[b * Q:(b + 1) * Q, 2, :, :].rearrange("p k f -> p (k f)")
                                   ).then_inc(out_stored, 16)
                pool.wait_ge(out_stored, (p + 1) * 16 * NB)

            gin_chunks(pool, store)

        @block.tensor
        def _(pe):
            pe.wait_ge(ident_ready, 1)
            pe.wait_ge(x_landed, 16 * NB)
            for g in range(NC):
                for k in range(K):
                    last = pe.transpose(ps[:, g, k * P:(k + 1) * P], xs[:, g * K + k, :], ident[:])
                last.then_inc(pe_pro, 1)
            pe.wait_ge(wext_ready, 1)
            for g in range(NC):
                pe.wait_ge(act_pro, g + 1)
                if g >= 4:
                    pe.wait_ge(act_pro, NC + g - 4 + 1)
                    pe.wait_ge(dve_pro, g - 4 + 1)
                if g == 0:
                    pe.wait_ge(act_pro, NC)
                for half in range(2):
                    bank = 2 * (g % 4) + half
                    for k in range(2):
                        t = g * K + 2 * half + k
                        last = pe.matmul(ps[:, bank, k * 256:k * 256 + F + 2 * H], xT[:, t * P:(t + 1) * P],
                                         wext[:], start=(k == 0), stop=(k == 1), skip_group_check=True)
                last.then_inc(pe_pro, 1)
            for g in range(NC):
                pe.wait_ge(act_pro, NC + 4 + g // 2 + 1)
                pe.wait_ge(dve_pro, 4 + g // 2 + 1)
                pe.matmul(ps[0:H, g, :], wext[:, F + H:F + 2 * H], xT[:, g * CH:(g + 1) * CH],
                          start=True, stop=True).then_inc(pe_pro, 1)
            pe.wait_ge(gin_w_landed, 16 * (2 * L + 6))
            pe.wait_ge(dve_pro, NC + 2)
            pe.wait_ge(act_pro, 2 * NC + 1)
            for j in range(2 * L + 2):
                last = pe.transpose(ps[:, j // 4, (j % 4) * P:(j % 4 + 1) * P], wraw[:, j, :], ident[:])
            last.then_inc(pe_pro, 1)
            pe.wait_ge(second_ready, 2 * H)
            pe.wait_ge(act_pro, 2 * NC + NC // 2 + 1)
            pe.wait_ge(dve_pro, NC + 1 + NC // 2)

            def attend(n, par):
                for c in range(NC):
                    m = n * NC + c
                    wait_apart(pe, [(b_ready, m + 1)])
                    for t in range(K):
                        if c == 0:
                            wait_apart(pe, [(act_evac, n * K + (t + 1 - K)),
                                            (dve_evac, n * K + (t + 1 - K))])
                        for k in range(K):
                            cols = slice(t * P, (t + 1) * P)
                            for h in range(H):
                                bank, at = (2 * t, h * HB) if h < 3 else (2 * t + 1, 0)
                                mm = pe.matmul(ps[:, bank, at:at + HB], ringf8[:, c % RING, h, cols, k],
                                               hv[:, c * K + k, h, :],
                                               start=(c == 0 and k == 0 and h in (0, 3)),
                                               stop=(c == NC - 1 and k == K - 1), skip_group_check=True)
                            if t == K - 1 and k == K - 1:
                                mm.then_inc(b_used, 1)
                            mm = pe.matmul(ps[:, 2 * t + 1, HB:HB + H * 2 * G], maskTf8[:, par, c, cols, k],
                                           hv[:, c * K + k, :, 2 * G:4 * G],
                                           start=False, stop=(c == NC - 1 and k == K - 1),
                                           skip_group_check=True)
                        if c == NC - 1:
                            mm.then_inc(acc_done, 1)

            attention_chunks(pe, attend)

            def layers(n):
                def layer(l):
                    for q in range(2):
                        pe.wait_ge(hid_ready, n * (2 * L + 2) + 2 * l + q + 1)
                        pe.matmul(ps[:, 4 + q, :], wt[:, q * L + l, :], hid[:, 2 * q + l % 2, :],
                                  start=True, stop=True).then_inc(mlp_done, 1)

                def merge():
                    pe.wait_ge(hid_ready, n * (2 * L + 2) + 2 * L + 2)
                    wait(pe, sum_ready, n)
                    for k in range(K):
                        for q in range(2):
                            mm = pe.matmul(ps[:, 6, k * F:(k + 1) * F],
                                           hid[:, 2 * q + L % 2, k * P:(k + 1) * P], wt[:, 2 * L + q, :],
                                           start=(k == 0 and q == 0), stop=(q == 1), skip_group_check=True)
                    mm.then_inc(merged, 1)
                return [lambda l=l: layer(l) for l in range(L)] + [merge]

            def add_neighbours(c, par, bank, operand_of, q, first, last):
                for k in range(K):
                    mm = pe.matmul(ps[:, bank, :], operand_of(c, q, k), maskTf8[:, par, c, :, k],
                                   start=(first and k == 0), stop=(last and k == K - 1))
                return mm

            def y_part(c, q, k):
                return ypart[:, c, q, k, :]

            def x2_part(c, q, k):
                return x2part[:, q, c * K + k, :]

            def gather(p, par, before, kept=False):
                work = layers(before) if before is not None else []
                if not kept:
                    wait_apart(pe, [(mask_landed[par], p * 8 - par * 8),
                                    (hid_ready, p * (2 * L + 2) + (2 - 2 * (2 * L + 2)))])
                for c in range(NC):
                    if kept:
                        wait_apart(pe, [(y_second, c + 1)])
                    for q in range(2):
                        mm = add_neighbours(c, par, 2 * par, y_part, q, c == 0 and q == 0,
                                            c == NC - 1 and q == 1)
                    if not kept:
                        for q in range(2):
                            mm = add_neighbours(c, par, 2 * par + 1, x2_part, q, c == 0 and q == 0,
                                                c == NC - 1 and q == 1)
                    if c == NC - 1:
                        mm.then_inc(gin_done, 1)
                    if work and c % 2 == 1:
                        work.pop(0)()

            pe.wait_ge(x2_second, 1)
            for p in range(KEPT):
                wait_apart(pe, [(dve_evac, NC * K - K + p + 1)])
                for c in range(NC):
                    for q in range(2):
                        add_neighbours(c, p, 2 * p + 1, x2_part, q, c == 0 and q == 0,
                                       c == NC - 1 and q == 1)
            wait_apart(pe, [(act_evac, NC * K), (dve_evac, NC * K)])
            gather(0, 0, None, kept=True)
            gather(1, 1, 0, kept=True)
            with pe.Fori(0, (NC - KEPT) // 2) as i:
                gather(i * 2 + 2, 0, i * 2 + 1)
                gather(i * 2 + 3, 1, i * 2 + 2)
            for step in layers(NC - 1):
                step()

        @block.scalar
        def _(act):
            for g in range(NC):
                act.wait_ge(pe_pro, g + 1)
                act.activation(xT[:, g * CH:(g + 1) * CH], ps[:, g, :], ACT.Copy).then_inc(act_pro, 1)
            for g in range(NC):
                act.wait_ge(pe_pro, NC + g + 1)
                for half in range(2):
                    t = g * K + 2 * half
                    last = act.activation(
                        gat[:, t:t + 2, :],
                        ps[:, 2 * (g % 4) + half, :].rearrange("p (k n) -> p k n", k=2)[:, :, 0:F], ACT.Copy)
                last.then_inc(act_pro, 1)
            for g in range(1, NC, 2):
                act.wait_ge(pe_pro, 2 * NC + g + 1)
                act.activation(s_rows[:, g * CH:(g + 1) * CH], ps[0:H, g, :], ACT.Copy).then_inc(act_pro, 1)
            act.wait_ge(exp_ready, 1)
            act.activation(vz[:, 0], ds[:, :, 0:H], ACT.Exp).then_inc(vz_ready, 1)
            act.activation(vz[:, 1], ds[:, :, 0:H], ACT.Exp, scale=SLOPE).then_inc(vz_ready, 1)
            act.wait_ge(exp_ready, 3)
            act.activation(uw[:, 0], uw[:, 0], ACT.Exp).then_inc(uw_ready, 1)
            act.activation(uw[:, 1], uw[:, 1], ACT.Exp, scale=-1.0).then_inc(uw_ready, 1)
            act.wait_ge(pe_pro, 3 * NC + 1)
            act.activation(wt[:].rearrange("p l n -> p (l n)"),
                           ps[:, 0:2, :].rearrange("p b n -> p (b n)"), ACT.Copy).then_inc(act_pro, 1)
            for j in range(2 * H):
                h, q = j // 2, j % 2
                if j in pool_share:
                    act.wait_ge(den_cols, pool_share.index(j) + 1)
                    act.wait_ge(pool_parts, pool_share.index(j) + 1)
                else:
                    act.wait_ge(den_cols_rest, mult_share.index(j) + 1)
                    act.wait_ge(dve_parts, mult_share.index(j) + 1)
                act.activation(hv[:, :, h, 2 * q * G:(2 * q + 1) * G], part[:, j % PARTS],
                               ACT.Copy, scale=1.0 / SPLIT).then_inc(first_ready, 1)
            act.wait_ge(second_ready, 2 * H)
            act.wait_ge(act_pro, 2 * NC + NC // 2 + 1)

            def elu_exponential(n):
                act.wait_ge(neg_ready, n + 1)
                act.activation(neg, neg, ACT.Exp).then_inc(elu_exp, 1)

            def evacuate(n):
                wait(act, combined, n)
                for t in range(K):
                    act.wait_ge(acc_done, n * K + (t + 1))
                    act.activation(sums[:, t, 0:BANK0], ps[:, 2 * t, 0:BANK0],
                                   ACT.Copy).then_inc(act_evac, 1)

            def compare(n, par):
                for c in range(NC):
                    m = n * NC + c
                    counts = [(b_used, m + (1 - RING))]
                    if c == 0:
                        counts.append((s_landed[par], (n + (2 - par)) * 8))
                    wait_apart(act, counts)
                    for k, h in act_share:
                        last = act.activation(ringf8[:, c % RING, h, :, k], s_all[:, par, h, :],
                                              ACT.Relu, bias=dbig[:, c * K + k, h:h + 1],
                                              scale=STEP_GAIN, saturate=False)
                    last.then_inc(act_steps, 1)
                    later = not (isinstance(n, int) and n == 0)
                    if c == 1 and later:
                        evacuate(n - 1)
                    if c == 5 and isinstance(n, int) and n == NC - 1:
                        act.wait_ge(x2_scale, 1)
                        act.activation(x2part[:, 0], x2raw, ACT.Copy, scale=x2top[:, 2:3]).then_inc(x2_first, 1)
                    if c == 6 and later:
                        elu_exponential(n - 1)

            attention_chunks(act, compare)
            evacuate(NC - 1)
            act.wait_ge(neg_rest, 1)
            elu_exponential(NC - 1)

            act.wait_ge(var_ready, 1)
            act.activation(std[:], var[:], ACT.Sqrt).then_inc(std_ready, 1)
            for c in range(NC):
                act.wait_ge(y_ready, c + 1)
                act.activation(ypart[:, c, 0], xs[:, c * K:(c + 1) * K, :], ACT.Copy,
                               scale=Y_GAIN).then_inc(y_first, 1)

            def gin_layers(n, c, par):
                act.wait_ge(gin_done, n + 1)
                for q in range(2):
                    wait(act, merged, n)
                    act.activation(hid[:, 2 * q, :], ps[:, 2 * par + q, :], ACT.Copy,
                                   scale=gain[:, q:q + 1]).then_inc(hid_ready, 1)
                for l in range(L):
                    for q in range(2):
                        act.wait_ge(mlp_done, n * 2 * L + 2 * l + q + 1)
                        act.activation(hid[:, 2 * q + (l + 1) % 2, :], ps[:, 4 + q, :], ACT.Relu,
                                       bias=bias[:, q * L + l:q * L + l + 1]).then_inc(hid_ready, 1)
                act.wait_ge(o_var, n + 1)
                act.activation(std[:, 0:K], moments[:, :, 1], ACT.Sqrt,
                               bias=ln_eps[:, 0:1]).then_inc(o_std, 1)

            gin_chunks(act, gin_layers)

        @block.vector
        def _(dve):
            links = [0]

            def link(ins):
                links[0] += 1
                ins.then_inc(chain, 1)
                dve.wait_ge(chain, links[0])

            dve.wait_ge(w_landed, 32)
            wv = wext[:, 0:F].rearrange("p (h f) -> p h f", h=H)
            for q, at in ((1, F), (0, F + H)):
                link(dve.tensor_tensor(w_a, wv, a_all[:, :, q * FH:(q + 1) * FH], ALU.mult))
                last = dve.tensor_reduce(wext[:, at:at + H], w_a, X, ALU.add)
                if q == 1:
                    link(last)
            last.then_inc(wext_ready, 1)
            dve.memset(ln_eps[:], LN_EPS)
            for g in range(NC):
                dve.wait_ge(act_pro, NC + g + 1)
                for half in range(2):
                    t = g * K + 2 * half
                    last = dve.tensor_copy(
                        ds[:, t:t + 2, :],
                        ps[:, 2 * (g % 4) + half, :].rearrange("p (k n) -> p k n", k=2)[:, :, F:F + 2 * H])
                last.then_inc(dve_pro, 1)
                dve.tensor_reduce(top_xw[:, g:g + 1], gat[:, g * K:(g + 1) * K, :].rearrange("p t f -> p (t f)"),
                                  X, ALU.max, apply_absolute_value=True).then_inc(xw_top, 1)
            dve.wait_ge(dve_pro, NC)
            dve.wait_ge(xw_top, NC)
            dve.tensor_reduce(top[:, H:H + 1], top_xw[:], X, ALU.max)
            dve.tensor_reduce(top[:, 0:H], ds[:, :, 0:H].rearrange("p t h -> p h t"), X,
                              ALU.max).then_inc(dve_pro, 1)
            for g in range(0, NC, 2):
                dve.wait_ge(pe_pro, 2 * NC + g + 1)
                dve.tensor_copy(s_rows[:, g * CH:(g + 1) * CH], ps[0:H, g, :]).then_inc(dve_pro, 1)
            dve.tensor_scalar(dneg[:], ds[:, :, 0:H], -1.0, None, ALU.mult)
            link(dve.tensor_scalar(dbig[:], ds[:, :, 0:H], STEP_GAIN, None, ALU.mult))

            def turn(n, par, t):
                s = n * K + t
                dve.wait_ge(adj_landed[t % 2], (n * 2 + (t // 2 + 1)) * 16 * NB)
                wait(dve, turned, s - 1)
                dve.tensor_scalar(mask[:, t % 2, :], rows[:, t % 2, :, :].rearrange("p b j -> p (b j)"),
                                  0.0, MASK_BYTE, ALU.is_gt, ALU.mult).then_inc(masked, 1)
                dve.wait_ge(masked, s + 1)
                dve.transpose(
                    maskT[:, par, :, t * P:(t + 1) * P].rearrange("p c (b i) -> p b c i", b=NB),
                    mask[:, t % 2, :].bitcast(I32).rearrange("p (b c w) -> p b c w", b=NB, w=Q)
                ).then_inc(turned, 1)

            turn(0, 0, 0)
            dve.wait_ge(topall_ready, 1)
            dall = topall[:, 0:H].unsqueeze(1).to_broadcast([P, NT, H])
            link(dve.tensor_tensor(ds[:, :, H:2 * H], ds[:, :, H:2 * H], dall, ALU.add))
            dve.tensor_tensor(ds[:, :, 0:H], ds[:, :, 0:H], dall, ALU.subtract).then_inc(exp_ready, 1)
            dve.tensor_scalar(uw[:, 0], ds[:, :, H:2 * H], 1.0 - SLOPE, 0.0, ALU.mult,
                              ALU.min).then_inc(exp_ready, 1)
            dve.tensor_scalar(uw[:, 1], ds[:, :, H:2 * H], 1.0 - SLOPE, 0.0, ALU.mult,
                              ALU.max).then_inc(exp_ready, 1)
            link(dve.tensor_scalar(topall[:, H:H + 1], topall[:, H:H + 1], 1e-30, None, ALU.max))
            link(dve.reciprocal(hscale[:], topall[:, H:H + 1]))
            dve.wait_ge(vz_ready, 2)
            link(dve.tensor_scalar(vz_den, vz, HP_TOP * SPLIT, None, ALU.mult))
            dve.tensor_scalar(vz, vz_den, hscale[:, 0:1], None, ALU.mult).then_inc(vz_scaled, 1)
            dve.wait_ge(vz_scaled, 1)
            dve.wait_ge(pe_pro, 3 * NC)
            operand(dve, mult_share[0], den_cols_rest, dve_parts)
            for j in range(2 * H):
                h, q = j // 2, j % 2
                if 0 < j < K:
                    turn(0, 0, j)
                dve.wait_ge(first_ready, j + 1)
                dve.scalar_tensor_tensor(
                    out=hv[:, :, h, (2 * q + 1) * G:(2 * q + 2) * G],
                    in0=hv[:, :, h, 2 * q * G:(2 * q + 1) * G], scalar=-SPLIT, in1=part[:, j % PARTS],
                    op0=ALU.mult, op1=ALU.add).then_inc(second_ready, 1)
                if j + PARTS in mult_share:
                    dve.wait_ge(second_ready, j + 1)
                    operand(dve, j + PARTS, den_cols_rest, dve_parts)

            def evacuate(n):
                wait(dve, combined, n)
                for t in range(K):
                    dve.wait_ge(acc_done, n * K + (t + 1))
                    dve.tensor_copy(sums[:, t, BANK0:ACC], ps[:, 2 * t + 1, 0:ACC - BANK0]).then_inc(dve_evac, 1)

            def reciprocals(n, tiles=tuple(range(K)), made=0):
                t0, t1 = tiles[0], tiles[-1] + 1
                dve.tensor_scalar(rden[:, t0:t1], full[:, t0:t1, :, 0, FH], hscale[:, 0:1], None,
                                  ALU.mult).then_inc(den_scaled, 1)
                dve.wait_ge(den_scaled, n + (1 + made))
                return dve.reciprocal(rden[:, t0:t1], rden[:, t0:t1])

            def row_statistics(n):
                for k in range(K):
                    last = dve.bn_stats(stats[:, bass.ds(n * K + k, 1), :].rearrange("p a s -> p (a s)"),
                                        xs[:, bass.ds(n * K + k, 1), :].rearrange("p a f -> p (a f)"))
                return last

            def mask_group(n, par, c):
                m = n * NC + c
                dve.wait_ge(act_steps, m + 1)
                dve.wait_ge(dve_steps, m + 1)
                dve.tensor_tensor(ring[:, c % RING], ring[:, c % RING],
                                  maskT[:, par, c:c + 1, :].to_broadcast([P, H, CH]),
                                  ALU.bitwise_and).then_inc(b_ready, 1)

            def compare(n, par):
                first, final = (isinstance(n, int) and n == m for m in (0, NC - 1))
                for c in range(NC):
                    m = n * NC + c
                    wait(dve, b_used, m + (1 - RING))
                    if c == 0:
                        dve.wait_ge(s_landed[par], (n + (2 - par)) * 8)
                        dve.wait_ge(turned, n * K + K)
                    for k, h in dve_share:
                        last = dve.tensor_scalar(ring8[:, c % RING, h, :, k], s_all[:, par, h, :],
                                                 dneg[:, c * K + k, h:h + 1], MASK_BYTE, ALU.is_gt, ALU.mult)
                    last.then_inc(dve_steps, 1)
                    if c > 0:
                        mask_group(n, par, c - 1)
                    if c == 1 and not first:
                        evacuate(n - 1)
                    if c == 4 and not first:
                        dve.wait_ge(den_ready, n)
                        reciprocals(n - 1).then_inc(rden_ready, 1)
                    if final and c == 1:
                        dve.wait_ge(x2_landed, 16 * NB)
                        dve.tensor_reduce(x2top[:, 0:1], x2raw.rearrange("p t f -> p (t f)"), X, ALU.max,
                                          apply_absolute_value=True).then_inc(x2_top, 1)
                    if final and c == 3:
                        dve.wait_ge(x2_topall, 1)
                        link(dve.tensor_scalar(x2top[:, 1:2], x2top[:, 1:2], 1e-30, None, ALU.max))
                        dve.tensor_scalar(x2top[:, 4:5], x2top[:, 1:2], 1.0 / (HP_TOP * MASK_ONE),
                                          None, ALU.mult)
                        link(dve.tensor_scalar(x2top[:, 3:4], x2top[:, 1:2], 1.0 / HP_TOP, None, ALU.mult))
                        dve.reciprocal(x2top[:, 2:3], x2top[:, 3:4]).then_inc(x2_scale, 1)
                    if final and c == 6:
                        dve.wait_ge(x2_first, 1)
                        dve.scalar_tensor_tensor(out=x2part[:, 1], in0=x2raw, scalar=x2top[:, 2:3],
                                                 in1=x2part[:, 0], op0=ALU.mult,
                                                 op1=ALU.subtract).then_inc(x2_second, 1)
                    if c % 2 == 1 and not final:
                        if c == 1:
                            wait(dve, acc_done, n * K)
                            wait(dve, mask_stored, n * 16)
                        turn(n + 1, 1 - par, c // 2)
                    if c == NC - 1 and not first:
                        dve.wait_ge(combined, n)
                        row_statistics(n - 1).then_inc(stats_ready, 1)
                mask_group(n, par, NC - 1)

            dve.wait_ge(act_pro, 2 * NC + NC // 2 + 1)
            dve.wait_ge(second_ready, 2 * H)
            attention_chunks(dve, compare)
            evacuate(NC - 1)

            dve.wait_ge(act_evac, NC * K)
            dve.wait_ge(dve_evac, NC * K)
            dve.wait_ge(uw_ready, 2)
            tiles = dve_tiles
            t0, t1 = tiles[0], K
            link(combine_sums(dve, NC - 1, tiles, link))
            link(reciprocals(NC - 1, tiles))
            link(attention_output(dve, NC - 1, tiles))
            dve.wait_ge(den_ready, NC)
            reciprocals(NC - 1, pool_tiles, 1).then_inc(rden_ready, 1)
            dve.tensor_scalar(neg[:, t0:t1], g_out[:, t0:t1], 0.0, None,
                              ALU.min).then_inc(neg_rest, 1)
            link(dve.tensor_scalar(g_out[:, t0:t1], g_out[:, t0:t1], 0.0, -1.0,
                                   ALU.max, ALU.add))
            link(dve.tensor_tensor(rows_of(xs, NC - 1, tiles), rows_of(xs, NC - 1, tiles),
                                   g_out[:, t0:t1], ALU.add))
            dve.wait_ge(elu_exp, NC)
            link(dve.tensor_tensor(rows_of(xs, NC - 1, tiles), rows_of(xs, NC - 1, tiles),
                                   neg[:, t0:t1], ALU.add))
            dve.wait_ge(combined, NC)
            row_statistics(NC - 1).then_inc(stats_ready, 1)
            dve.wait_ge(stats_ready, NC)

            dve.tensor_tensor(mean[:], stats[:, :, 1], stats[:, :, 4], ALU.add)
            dve.tensor_tensor(spread[:], stats[:, :, 1], stats[:, :, 4], ALU.subtract)
            link(dve.tensor_tensor(var[:], stats[:, :, 2], stats[:, :, 5], ALU.add))
            dve.tensor_scalar(mean[:], mean[:], 0.5, None, ALU.mult)
            dve.tensor_tensor(spread[:], spread[:], spread[:], ALU.mult)
            link(dve.tensor_scalar(var[:], var[:], 1.0 / F, LN_EPS, ALU.mult, ALU.add))
            dve.scalar_tensor_tensor(out=var[:], in0=spread[:], scalar=0.25, in1=var[:], op0=ALU.mult,
                                     op1=ALU.add).then_inc(var_ready, 1)
            dve.wait_ge(gin_w_landed, 16 * (2 * L + 6))
            dve.tensor_scalar(gain[:, 0:1], eps_all[:, 0:1], 2.0, 1.0 / (Y_GAIN * MASK_ONE), ALU.add, ALU.mult)
            dve.tensor_scalar(gain[:, 1:2], eps_all[:, 1:2], 2.0, x2top[:, 4:5], ALU.add, ALU.mult)
            dve.wait_ge(std_ready, 1)
            link(dve.reciprocal(rstd[:], std[:]))

            def y_rest(c):
                dve.wait_ge(y_first, c + 1)
                dve.scalar_tensor_tensor(out=ypart[:, c, 1], in0=xs[:, c * K:(c + 1) * K, :], scalar=Y_GAIN,
                                         in1=ypart[:, c, 0], op0=ALU.mult,
                                         op1=ALU.subtract).then_inc(y_second, 1)

            for c in range(NC):
                for t in range(c * K, (c + 1) * K):
                    last = dve.tensor_scalar(xs[:, t, :], xs[:, t, :], mean[:, t:t + 1], rstd[:, t:t + 1],
                                             ALU.subtract, ALU.mult)
                last.then_inc(y_ready, 1)
                if c > 0:
                    y_rest(c - 1)
            y_rest(NC - 1)
            dve.wait_ge(y_second, NC)
            link(dve.tensor_tensor(xs[:], xs[:], bm_all[:].unsqueeze(1).to_broadcast([P, NT, F]), ALU.add))

            def finish(n, c, par):
                cen, o = res[:, 0], res[:, 2]
                base = links[0]
                wait(dve, o_ready, n)
                dve.wait_ge(merged, n + 1)
                dve.tensor_tensor(cen, ps[:, 6, :].rearrange("p (k f) -> p k f", k=K),
                                  xs[:, bass.ds(c * K, K), :], ALU.add).then_inc(sum_ready, 1)
                dve.wait_ge(sum_ready, n + 1)
                for k in range(K):
                    last = dve.bn_stats(stats[:, k, :], cen[:, k, :])
                last.then_inc(chain, 1)
                wait_apart(dve, [(chain, n * 2 + (base + 1))])
                for k in range(K):
                    last = dve.bn_aggr(moments[:, k, :], stats[:, k, :])
                last.then_inc(o_var, 1)
                dve.wait_ge(o_std, n + 1)
                dve.reciprocal(rstd[:, 0:K], std[:, 0:K]).then_inc(chain, 1)
                dve.wait_ge(chain, n * 2 + (base + 2))
                wait(dve, out_stored, n * (16 * NB))
                for k in range(K):
                    last = dve.tensor_scalar(o[:, k, :], cen[:, k, :], moments[:, k, 0:1], rstd[:, k:k + 1],
                                             ALU.subtract, ALU.mult)
                last.then_inc(o_ready, 1)

            gin_chunks(dve, finish)


_INS = ['x', 'adj', 'L0_gnn_W', 'L0_gnn_a', 'L1_gnn_x2', 'L1_gnn_eps1', 'L1_gnn_eps2', 'L1_gnn_W1',
        'L1_gnn_b1', 'L1_gnn_W2', 'L1_gnn_b2', 'L1_gnn_Wm', 'L1_gnn_bm']
_OUTS = [((4096, 128), 'float32')]


def kernel(**inputs):
    import numpy as _np
    import concourse.bacc as _bacc
    from concourse import mybir as _mybir
    from concourse.bass_utils import run_bass_kernel_spmd as _run

    nc = _bacc.Bacc("TRN2", target_bir_lowering=False, num_devices=1)
    arrays, args = {}, []
    for name in _INS:
        a = _np.ascontiguousarray(inputs[name])
        arrays[f"in_{name}_dram"] = a
        args.append(nc.dram_tensor(f"in_{name}_dram", a.shape, _mybir.dt.from_np(a.dtype), kind="ExternalInput").ap())
    for i, (shape, dtype) in enumerate(_OUTS):
        dt = _mybir.dt.from_np(_np.dtype(dtype))
        args.append(nc.dram_tensor(f"out_{i}_dram", shape, dt, kind="ExternalOutput").ap())
    gat_gin_resnorm_kernel(nc, *args)
    r = _run(nc, [arrays], core_ids=[0])
    got = tuple(r.results[0][f"out_{i}_dram"] for i in range(len(_OUTS)))
    return got[0]
```

```python
from contextlib import ExitStack

import concourse.bass as bass
from concourse import mybir

F32 = mybir.dt.float32
F16 = mybir.dt.float16
F8 = mybir.dt.float8e4
U8 = mybir.dt.uint8
I32 = mybir.dt.int32
ALU = mybir.AluOpType
ACT = mybir.ActivationFunctionType
X = mybir.AxisListType.X
RMAX = bass.bass_isa.ReduceOp.max

P = 128
Q = 32
NB = P // Q
K = 4
MASK_BYTE = 64.0
MASK_ONE = 2.0
STEP_GAIN = 2.0 ** 60
HP_TOP = 2.0 ** 15
Y_GAIN = 2.0 ** 10
RING = 4
PARTS = 3
ACT_STEPS = 10
ACT_FIRST = 9
EARLY = 2
SLOPE = 0.2
LN_EPS = 1e-5


def gat_gin_resnorm_kernel(nc, x, adj, w, a, x2, eps1, eps2, w1, b1, w2, b2, wm, bm, out):
    N, F = x.shape
    H, FH = a.shape[0], a.shape[1] // 2
    NT = N // P
    NC = NT // K
    CH = K * P
    JB = N // NB
    G = FH + 1
    HB = 4 * G
    AZ = H * HB
    AX = AZ + H * G
    ACC = AX + F
    BANK0 = 3 * HB
    L = w1.shape[0]

    with ExitStack() as ctx:
        def sb(name, shape, dt):
            return ctx.enter_context(nc.sbuf_tensor(name, shape, dt))

        def sem(name):
            return ctx.enter_context(nc.semaphore(name))

        KEPT = 2
        s_dram = nc.dram_tensor("s_rows", [H, N], F32).ap()
        mask_dram = nc.dram_tensor("mask_words", [NC - KEPT, P, NC * CH], I32).ap()
        x2s_dram = nc.dram_tensor("x2_sums", [NC, P, K * F], F32).ap()

        xs = sb("xs", [P, NT, F], F32)
        parts = sb("parts", [P, NT, 2, 2 * H * G + F], F16)
        rows = sb("rows", [P, 2, NB, JB], F32)
        mask = sb("mask", [P, 2, NB * JB], U8)
        maskT = sb("maskT", [P, 2, NC, CH], I32)
        ring = sb("ring", [P, RING, H, CH], I32)
        s_all = sb("s_all", [P, 2, H, CH], F32)
        sums = sb("sums", [P, K, ACC], F32)
        ident = sb("ident", [P, P], F32)
        wext = sb("wext", [P, F + 2 * H], F32)
        ds = sb("ds", [P, NT, 2 * H], F32)
        dneg = sb("dneg", [P, NT, H], F32)
        dbig = sb("dbig", [P, NT, H], F32)
        uw = sb("uw", [P, 2, NT, H], F32)
        top = sb("top", [P, H + 1], F32)
        topall = sb("topall", [P, H + 1], F32)
        top_xw = sb("top_xw", [P, NC], F32)
        hscale = sb("hscale", [P, 1], F32)
        rden = sb("rden", [P, K, H], F32)
        x2top = sb("x2top", [P, 5], F32)
        wt = sb("wt", [P, 2 * L + 2, P], F32)
        bias = sb("bias", [P, 2 * L], F32)
        bm_all = sb("bm_all", [P, F], F32)
        gain = sb("gain", [P, 2], F32)
        eps_all = sb("eps_all", [P, 2], F32)
        stats = sb("stats", [P, NT, 6], F32)
        moments = sb("moments", [P, K, 2], F32)
        mean = sb("mean", [P, NT], F32)
        spread = sb("spread", [P, NT], F32)
        var = sb("var", [P, NT], F32)
        std = sb("std", [P, NT], F32)
        ln_eps = sb("ln_eps", [P, 1], F32)
        rstd = sb("rstd", [P, NT], F32)
        ps = ctx.enter_context(nc.psum_tensor("ps", [P, 8, 512], F32))

        flat_ring = ring[:].rearrange("p r h i -> p (r h i)").bitcast(F32)
        vz_part = parts[:, :, :, 0:2 * H * G].rearrange("p t r (q h g) -> p t r q h g", q=2, h=H)
        head_parts = parts[:, :, :, 0:2 * H * G].rearrange("p t r (q h g) -> p t h q r g", q=2, h=H)
        z_x2_part = parts[:, :, :, H * G:2 * H * G + F]
        x2part = parts[:, :, :, 2 * H * G:2 * H * G + F].rearrange("p t r f -> p r t f")
        flat_parts = parts[:].rearrange("p t r n -> p (t r n)").bitcast(F32)
        xT = flat_parts[:, 0:N]
        wraw = flat_parts[:, N:N + (2 * L + 2) * P].rearrange("p (l n) -> p l n", n=P)
        x2raw = flat_ring[:, RING * H * CH - NT * F:].rearrange("p (t f) -> p t f", f=F)
        xw = maskT[:, 1].bitcast(F32).rearrange("p c i -> p (c i)").rearrange(
            "p (t f) -> p t f", f=F)
        s_rows = s_all[:].rearrange("p r h i -> p (r h i)")[0:H, :]
        flat_sums = sums[:].rearrange("p t n -> p (t n)")
        w_a = flat_sums[:, 0:F].rearrange("p (h f) -> p h f", h=H)
        a_all = flat_sums[:, F:F + H * 2 * FH].rearrange("p (h f) -> p h f", h=H)
        vz = flat_sums[:, ACC * K - 2 * NT * H:ACC * K].rearrange("p (q t h) -> p q t h", q=2, h=H)
        vz_den = flat_sums[:, ACC * K - 4 * NT * H:ACC * K - 2 * NT * H].rearrange(
            "p (q t h) -> p q t h", q=2, h=H)
        own = F + H * 2 * FH
        part = [place.rearrange("p (t g) -> p t g", g=G) for place in (
            flat_sums[:, own:own + NT * G], flat_sums[:, own + NT * G:own + 2 * NT * G],
            flat_ring[:, H * CH:H * CH + NT * G])]
        ypart = rows[:, 0].rearrange("p b j -> p (b j)").bitcast(F16).rearrange(
            "p (c q k f) -> p c q k f", q=2, k=K, f=F)
        x2s = rows[:, 1].rearrange("p b j -> p (b j)")[:, 0:2 * K * F].rearrange(
            "p (r k f) -> p r k f", r=2, f=F)
        hid = s_all[:].rearrange("p r h i -> p (r h) i")
        res = flat_sums[:, 0:3 * K * F].rearrange("p (r k f) -> p r k f", r=3, f=F)

        ring8 = ring[:].rearrange("p r h i -> p (r h i)").bitcast(U8).rearrange(
            "p (r h i k) -> p r h i k", r=RING, h=H, k=K)
        ringf8 = ring[:].rearrange("p r h i -> p (r h i)").bitcast(F8).rearrange(
            "p (r h i k) -> p r h i k", r=RING, h=H, k=K)
        maskTf8 = maskT[:].rearrange("p r c i -> p (r c i)").bitcast(F8).rearrange(
            "p (r c i k) -> p r c i k", r=2, c=NC, k=K)

        x_v = x.rearrange("(b c w k) f -> b w c (k f)", b=NB, c=NC, w=Q)
        x2_v = x2.rearrange("(b c w k) f -> b w c (k f)", b=NB, c=NC, w=Q)
        out_v = out.rearrange("(b c w k) f -> c b w (k f)", b=NB, c=NC, w=Q)
        adj_v = adj.rearrange("(B c w k) (b j) -> c k b w B j", B=NB, c=NC, w=Q, b=NB)
        ring_v = [ring[:, 2 * r:2 * r + 2].rearrange("p r h i -> p (r h i)") for r in range(2)]
        ringTf8 = [ring_v[r].bitcast(F8).rearrange("p (c i k) -> p c i k", c=NC, k=K) for r in range(2)]
        gin_masks = [maskTf8[:, r] for r in range(2)] + ringTf8
        mask_v = [maskT[:, r].rearrange("p c i -> p (c i)") for r in range(2)]
        s_v = s_dram.rearrange("h (c i) -> c h i", i=CH)

        x_landed = sem("x_landed")
        w_landed = sem("w_landed")
        gin_w_landed = sem("gin_w_landed")
        x2_landed = sem("x2_landed")
        adj_landed = [sem(f"adj_landed{r}") for r in range(2)]
        s_stored = sem("s_stored")
        xw_top = sem("xw_top")
        s_landed = [sem(f"s_landed{r}") for r in range(2)]
        mask_stored = sem("mask_stored")
        x2s_stored = sem("x2s_stored")
        x2s_landed = [sem(f"x2s_landed{r}") for r in range(2)]
        ring_landed = sem("ring_landed")
        mask_landed = [sem(f"mask_landed{r}") for r in range(2)]
        out_stored = sem("out_stored")
        ident_zero = sem("ident_zero")
        ident_ready = sem("ident_ready")
        topall_ready = sem("topall_ready")
        wext_ready = sem("wext_ready")
        pe_pro = sem("pe_pro")
        act_pro = sem("act_pro")
        dve_pro = sem("dve_pro")
        chain = sem("chain")
        vz_ready = sem("vz_ready")
        uw_ready = sem("uw_ready")
        exp_ready = sem("exp_ready")
        vz_scaled = sem("vz_scaled")
        part_ready = sem("part_ready")
        den_cols = sem("den_cols")
        first_ready = sem("first_ready")
        second_ready = sem("second_ready")
        masked = sem("masked")
        turned = sem("turned")
        act_steps = sem("act_steps")
        dve_steps = sem("dve_steps")
        b_ready = sem("b_ready")
        b_used = sem("b_used")
        acc_done = sem("acc_done")
        act_evac = sem("act_evac")
        dve_evac = sem("dve_evac")
        g_chain = sem("g_chain")
        den_ready = sem("den_ready")
        rden_ready = sem("rden_ready")
        combined = sem("combined")
        neg_ready = sem("neg_ready")
        neg_rest = sem("neg_rest")
        x_added = sem("x_added")
        den_scaled = sem("den_scaled")
        elu_exp = sem("elu_exp")
        stats_ready = sem("stats_ready")
        var_ready = sem("var_ready")
        std_ready = sem("std_ready")
        y_ready = sem("y_ready")
        y_first = sem("y_first")
        y_second = sem("y_second")
        x2_top = sem("x2_top")
        x2_topall = sem("x2_topall")
        x2_scale = sem("x2_scale")
        x2_first = sem("x2_first")
        x2_second = sem("x2_second")
        gin_done = sem("gin_done")
        hid_ready = sem("hid_ready")
        mlp_done = sem("mlp_done")
        merged = sem("merged")
        sum_ready = sem("sum_ready")
        o_var = sem("o_var")
        o_std = sem("o_std")
        o_ready = sem("o_ready")
        passed = sem("passed")

        def wait(eng, s, value):
            if not isinstance(value, int) or value > 0:
                eng.wait_ge(s, value)

        def wait_apart(eng, counts):
            for q, v in counts:
                wait(eng, q, v)
            eng.sem_inc(passed, 1)

        def attention_chunks(eng, chunk):
            chunk(0, 0)
            chunk(1, 1)
            with eng.Fori(0, (NC - 4) // 2) as i:
                chunk(i * 2 + 2, 0)
                chunk(i * 2 + 3, 1)
            chunk(NC - 2, 0)
            chunk(NC - 1, 1)

        def s_there(n, par):
            return s_landed[par], (n + (2 - par)) * 8

        def gin_chunks(eng, step):
            for p in range(KEPT):
                step(p, NC - KEPT + p, p)
            with eng.Fori(0, (NC - KEPT) // 2) as i:
                step(i * 2 + 2, i * 2, 0)
                step(i * 2 + 3, i * 2 + 1, 1)

        full = sums[:, :, 0:H * HB].rearrange("p t (h q g) -> p t h q g", h=H, q=4)
        az = sums[:, :, AZ:AX].rearrange("p t (h g) -> p t h g", h=H)
        g_out = full[:, :, :, 1, 0:FH]
        neg = full[:, :, :, 2, 0:FH]

        def combine_sums(eng, n, tiles, settle):
            for t in tiles:
                last = eng.tensor_tensor(full[:, t, :, 0:4:2, :], full[:, t, :, 0:4:2, :],
                                         full[:, t, :, 1:4:2, :], ALU.add)
            settle(last)
            t0, t1 = tiles[0], tiles[-1] + 1
            settle(eng.tensor_tensor(full[:, t0:t1, :, 2, :], az[:, t0:t1], full[:, t0:t1, :, 2, :],
                                     ALU.subtract))
            for q in range(2):
                last = eng.tensor_tensor(
                    full[:, t0:t1, :, 2 * q, :], full[:, t0:t1, :, 2 * q, :],
                    uw[:, q, bass.ds(n * K + t0, t1 - t0), :].unsqueeze(3).to_broadcast(
                        [P, t1 - t0, H, G]), ALU.mult)
            settle(last)
            return eng.tensor_tensor(full[:, t0:t1, :, 0, :], full[:, t0:t1, :, 0, :],
                                     full[:, t0:t1, :, 2, :], ALU.add)

        def rows_of(buf, n, tiles):
            return buf[:, bass.ds(n * K + tiles[0], len(tiles)), :].rearrange("p t (h g) -> p t h g", h=H)

        def attention_output(eng, n, tiles):
            t0, t1 = tiles[0], tiles[-1] + 1
            return eng.tensor_tensor(g_out[:, t0:t1], full[:, t0:t1, :, 0, 0:FH],
                                     rden[:, t0:t1].unsqueeze(3).to_broadcast([P, t1 - t0, H, FH]), ALU.mult)

        steps = [(k, h) for k in range(K) for h in range(H)]

        def act_count(n, c):
            if not (isinstance(n, int) and n == 0):
                return ACT_STEPS
            return len(steps) if c == 0 else ACT_FIRST if c < NC - K else ACT_STEPS

        pool_tiles, dve_tiles = (0,), tuple(range(1, K))

        def operand(eng, j):
            h, q = j // 2, j % 2
            eng.tensor_copy(part[j % PARTS][:, :, FH], vz_den[:, q, :, h]).then_inc(den_cols, 1)
            eng.tensor_tensor(part[j % PARTS][:, :, 0:FH], xw[:, :, h * FH:(h + 1) * FH],
                              vz[:, q, :, h:h + 1].to_broadcast([P, NT, FH]),
                              ALU.mult).then_inc(part_ready, 1)

        block = ctx.enter_context(nc.Block())

        @block.sync
        def _(sp):
            sp.dma_start(wext[:, 0:F], w).then_inc(w_landed, 16)
            sp.dma_start(a_all, a.partition_broadcast(P)).then_inc(w_landed, 16)
            for b in range(NB):
                sp.dma_start(xs[b * Q:(b + 1) * Q, :, :].rearrange("p (c k) f -> p c (k f)", k=K),
                             x_v[b]).then_inc(x_landed, 16)

            def load_tile(c, t):
                for b in (0, 2, 1, 3):
                    sp.dma_start(rows[b * Q:(b + 1) * Q, t % 2, :, :],
                                 adj_v[c, t, b]).then_inc(adj_landed[t % 2], 16)

            def load_s(n, par):
                sp.dma_start(s_all[:, par, :, :], s_v[n].partition_broadcast(P)).then_inc(s_landed[par], 16)

            def store_x2_sums(n):
                sp.wait_ge(dve_evac, n * K + K)
                sp.dma_start(x2s_dram[n].rearrange("p (k f) -> p k f", k=K),
                             sums[:, :, AX:ACC]).then_inc(x2s_stored, 16)

            def load_chunk(n, par):
                early, last = (isinstance(n, int) and n == m for m in (1, NC - 1))
                for t in range(K):
                    if t == 2 and not last:
                        sp.wait_ge(turned, n * K)
                        sp.dma_start(mask_dram[n - 1], mask_v[1 - par]).then_inc(mask_stored, 16)
                    if t == 2 and not early:
                        sp.wait_ge(act_steps, (n - 1) * NC)
                        sp.wait_ge(dve_steps, (n - 1) * NC)
                        load_s(n, par)
                        store_x2_sums(n - 2)
                    sp.wait_ge(masked, n * K + t - 1)
                    load_tile(n, t)

            for b in range(NB):
                sp.dma_start(x2raw[b * Q:(b + 1) * Q, :, :].rearrange("p (c k) f -> p c (k f)", k=K),
                             x2_v[b]).then_inc(x2_landed, 16)
            load_tile(0, 0)
            load_tile(0, 1)
            for l in range(L):
                sp.dma_start(wraw[:, l, :], w1[l]).then_inc(gin_w_landed, 16)
                sp.dma_start(wraw[:, L + l, :], w2[l]).then_inc(gin_w_landed, 16)
            sp.dma_start(wraw[:, 2 * L:2 * L + 2, :],
                         wm.rearrange("o (q i) -> o q i", q=2)).then_inc(gin_w_landed, 16)
            with nc.allow_non_contiguous_dma("a bias per partition"):
                sp.dma_start(bias[:, 0:L], b1.rearrange("l f -> f l")).then_inc(gin_w_landed, 16)
                sp.dma_start(bias[:, L:2 * L], b2.rearrange("l f -> f l")).then_inc(gin_w_landed, 16)
            sp.dma_start(bm_all[:], bm.partition_broadcast(P)).then_inc(gin_w_landed, 16)
            sp.dma_start(eps_all[:, 0:1], eps1.partition_broadcast(P)).then_inc(gin_w_landed, 16)
            sp.dma_start(eps_all[:, 1:2], eps2.partition_broadcast(P)).then_inc(gin_w_landed, 16)
            sp.wait_ge(s_stored, 16)
            load_s(0, 0)
            for t in (2, 3):
                sp.wait_ge(masked, t - 1)
                load_tile(0, t)
            load_s(1, 1)
            load_chunk(1, 1)
            with sp.Fori(0, (NC - 4) // 2) as i:
                load_chunk(i * 2 + 2, 0)
                load_chunk(i * 2 + 3, 1)
            load_chunk(NC - 2, 0)
            load_chunk(NC - 1, 1)
            sp.wait_ge(masked, NC * K)

            def load_x2_sums(c, r):
                sp.dma_start(x2s[:, r].rearrange("p k f -> p (k f)"), x2s_dram[c]).then_inc(x2s_landed[r], 16)

            def store(p, c):
                sp.wait_ge(o_ready, p + 1)
                for b in range(NB):
                    sp.dma_start(out_v[c, b], res[b * Q:(b + 1) * Q, 2, :, :].rearrange("p k f -> p (k f)")
                                 ).then_inc(out_stored, 16)

            store_x2_sums(NC - 2)
            sp.wait_ge(x2s_stored, 16 * (NC - KEPT + 1))
            load_x2_sums(NC - KEPT, 0)
            sp.wait_ge(mask_stored, 16 * (NC - KEPT))
            sp.wait_ge(b_used, NC * NC)
            for r in range(2):
                sp.dma_start(ring_v[r], mask_dram[r]).then_inc(ring_landed, 16)
            store_x2_sums(NC - 1)
            sp.wait_ge(x2s_stored, 16 * NC)
            load_x2_sums(NC - 1, 1)
            for r in range(2):
                sp.wait_ge(gin_done, r + 1)
                load_x2_sums(r, r)
            store(0, NC - KEPT)
            sp.wait_ge(gin_done, 3)
            sp.dma_start(mask_v[0], mask_dram[2]).then_inc(mask_landed[0], 16)
            load_x2_sums(2, 0)
            store(1, NC - 1)
            sp.wait_ge(gin_done, 4)
            sp.dma_start(mask_v[1], mask_dram[3]).then_inc(mask_landed[1], 16)
            load_x2_sums(3, 1)
            store(2, 0)
            for p in (6, 7):
                sp.wait_ge(gin_done, p - 1)
                sp.dma_start(mask_v[p % 2], mask_dram[p - KEPT]).then_inc(mask_landed[p % 2], 16)
                load_x2_sums(p - KEPT, p % 2)
                store(p - 3, p - 3 - KEPT)
            with sp.Fori(5, NC) as p:
                store(p, p - KEPT)
            sp.wait_ge(out_stored, NC * 16 * NB)

        @block.gpsimd
        def _(pool):
            pool.memset(ident[:], 0.0).then_inc(ident_zero, 1)
            pool.wait_ge(ident_zero, 1)
            pool.affine_select(out=ident[:], in_=ident[:], compare_op=ALU.not_equal, fill=1.0, base=0,
                               pattern=[[-1, P]], channel_multiplier=1).then_inc(ident_ready, 1)
            pool.wait_ge(x2_top, 1)
            pool.partition_all_reduce(x2top[:, 1:2], x2top[:, 0:1], P, RMAX).then_inc(x2_topall, 1)
            pool.wait_ge(dve_pro, NC + 1)
            pool.partition_all_reduce(topall[:], top[:], P, RMAX).then_inc(topall_ready, 1)
            pool.wait_ge(vz_scaled, 1)
            pool.wait_ge(pe_pro, 3 * NC)
            for j in range(2 * H):
                wait(pool, second_ready, j + 1 - PARTS)
                operand(pool, j)

            def combine(n, tiles=tuple(range(K))):
                base = n * 5
                made = [0]

                def settle(ins):
                    ins.then_inc(g_chain, 1)
                    made[0] += 1
                    wait_apart(pool, [(g_chain, base + made[0])])

                pool.wait_ge(act_evac, n * K + K)
                pool.wait_ge(dve_evac, n * K + K)
                combine_sums(pool, n, tiles, settle).then_inc(den_ready, 1)
                pool.wait_ge(den_ready, n + 1)
                pool.wait_ge(rden_ready, n + 1)
                settle(attention_output(pool, n, tiles))
                t0, t1 = tiles[0], tiles[-1] + 1
                pool.tensor_scalar(neg[:, t0:t1], g_out[:, t0:t1], 0.0, None,
                                   ALU.min).then_inc(neg_ready, 1)
                settle(pool.tensor_scalar(g_out[:, t0:t1], g_out[:, t0:t1], 0.0, -1.0,
                                          ALU.max, ALU.add))
                pool.tensor_tensor(rows_of(xs, n, tiles), rows_of(xs, n, tiles), g_out[:, t0:t1],
                                   ALU.add).then_inc(x_added, 1)
                wait_apart(pool, [(x_added, n + 1), (elu_exp, n + 1)])
                pool.tensor_tensor(rows_of(xs, n, tiles), rows_of(xs, n, tiles), neg[:, t0:t1],
                                   ALU.add).then_inc(combined, 1)

            pool.wait_ge(uw_ready, 2)
            combine(0)
            combine(1)
            with pool.Fori(2, NC - 2) as n:
                combine(n)
            combine(NC - 2)
            combine(NC - 1, pool_tiles)

        @block.tensor
        def _(pe):
            pe.wait_ge(ident_ready, 1)
            pe.wait_ge(x_landed, 16 * NB)
            for g in range(NC):
                for k in range(K):
                    last = pe.transpose(ps[:, g, k * P:(k + 1) * P], xs[:, g * K + k, :], ident[:])
                last.then_inc(pe_pro, 1)
            pe.wait_ge(wext_ready, 1)
            for g in range(NC):
                pe.wait_ge(act_pro, g + 1)
                if g >= 4:
                    pe.wait_ge(act_pro, NC + g - 4 + 1)
                    pe.wait_ge(dve_pro, g - 4 + 1)
                if g == 0:
                    pe.wait_ge(act_pro, NC)
                for half in range(2):
                    bank = 2 * (g % 4) + half
                    for k in range(2):
                        t = g * K + 2 * half + k
                        last = pe.matmul(ps[:, bank, k * 256:k * 256 + F + 2 * H], xT[:, t * P:(t + 1) * P],
                                         wext[:], start=(k == 0), stop=(k == 1), skip_group_check=True)
                last.then_inc(pe_pro, 1)
            for g in range(NC):
                pe.wait_ge(act_pro, NC + 4 + g // 2 + 1)
                pe.wait_ge(dve_pro, 4 + g // 2 + 1)
                pe.matmul(ps[0:H, g, :], wext[:, F + H:F + 2 * H], xT[:, g * CH:(g + 1) * CH],
                          start=True, stop=True).then_inc(pe_pro, 1)
            pe.wait_ge(gin_w_landed, 16 * (2 * L + 6))
            pe.wait_ge(act_pro, 2 * NC + 2)
            for j in range(2 * L + 2):
                last = pe.transpose(ps[:, j // 4, (j % 4) * P:(j % 4 + 1) * P], wraw[:, j, :], ident[:])
            last.then_inc(pe_pro, 1)
            pe.wait_ge(act_pro, 3 * NC + 1)

            def add_x2(par, t, c, k, start, stop):
                for q in range(2):
                    mm = pe.matmul(ps[:, 2 * t + 1, HB + H * G:HB + H * G + F],
                                   maskTf8[:, par, c, t * P:(t + 1) * P, k], x2part[:, q, c * K + k, :],
                                   start=(start and q == 0), stop=stop, skip_group_check=True)
                return mm

            wait_apart(pe, [(x2_second, 1)])
            for t in range(K):
                wait_apart(pe, [(turned, t + 1)])
                for c in range(NC):
                    for k in range(K):
                        add_x2(0, t, c, k, c == 0 and k == 0, c == NC - 1 and k == K - 1)
            pe.wait_ge(second_ready, 2 * H)

            def attend(n, par):
                first = isinstance(n, int) and n == 0
                for c in range(NC):
                    m = n * NC + c
                    wait_apart(pe, [(b_ready, m + 1)])
                    for t in range(K):
                        if c == 0:
                            wait_apart(pe, [(act_evac, n * K + (t + 1 - K)),
                                            (dve_evac, n * K + (t + 1 - K))])
                        for k in range(K):
                            cols = slice(t * P, (t + 1) * P)
                            for h in range(H):
                                bank, at = (2 * t, h * HB) if h < 3 else (2 * t + 1, 0)
                                mm = pe.matmul(ps[:, bank, at:at + HB], ringf8[:, c % RING, h, cols, k],
                                               head_parts[:, c * K + k, h],
                                               start=(c == 0 and k == 0 and
                                                      (h == 0 or h == 3 and not first)),
                                               stop=(c == NC - 1 and k == K - 1), skip_group_check=True)
                            if t == K - 1 and k == K - 1:
                                mm.then_inc(b_used, 1)
                            done = c == NC - 1 and k == K - 1
                            width = H * G if first else H * G + F
                            for r in range(2):
                                mm = pe.matmul(ps[:, 2 * t + 1, HB:HB + width],
                                               maskTf8[:, par, c, cols, k],
                                               z_x2_part[:, c * K + k, r, 0:width],
                                               start=False, stop=done, skip_group_check=True)
                        if c == NC - 1:
                            mm.then_inc(acc_done, 1)

            attention_chunks(pe, attend)

            def layers(n):
                def layer(l):
                    for q in range(2):
                        pe.wait_ge(hid_ready, n * (2 * L + 2) + 2 * l + q + 1)
                        pe.matmul(ps[:, 4 + q, :], wt[:, q * L + l, :], hid[:, 2 * q + l % 2, :],
                                  start=True, stop=True).then_inc(mlp_done, 1)

                def merge():
                    pe.wait_ge(hid_ready, n * (2 * L + 2) + 2 * L + 2)
                    wait(pe, sum_ready, n)
                    for k in range(K):
                        for q in range(2):
                            mm = pe.matmul(ps[:, 6, k * F:(k + 1) * F],
                                           hid[:, 2 * q + L % 2, k * P:(k + 1) * P], wt[:, 2 * L + q, :],
                                           start=(k == 0 and q == 0), stop=(q == 1), skip_group_check=True)
                    mm.then_inc(merged, 1)
                return [lambda l=l: layer(l) for l in range(L)] + [merge]

            def add_neighbours(c, par, masks):
                for k in range(K):
                    for q in range(2):
                        pe.matmul(ps[:, 2 * par, :], ypart[:, c, q, k, :], masks[:, c, :, k],
                                  start=(c == 0 and k == 0 and q == 0),
                                  stop=(c == NC - 1 and k == K - 1 and q == 1))

            def turn_x2_sums(p, par):
                pe.wait_ge(x2s_landed[par], p * 8 + (16 - 8 * par))
                for k in range(K):
                    mm = pe.transpose(ps[:, 2 * par + 1, k * P:(k + 1) * P], x2s[:, par, k, :], ident[:])
                mm.then_inc(gin_done, 1)

            def gather(p, par, masks, landed, work, every):
                wait_apart(pe, [landed,
                                (hid_ready, p * (2 * L + 2) + (2 - 2 * (2 * L + 2)))])
                for c in range(NC):
                    add_neighbours(c, par, masks)
                    if work and c % every == every - 1:
                        work.pop(0)()
                turn_x2_sums(p, par)

            for p in range(KEPT):
                wait_apart(pe, [(act_evac, NC * K - K + p + 1)])
                for c in range(NC - 1):
                    wait_apart(pe, [(y_second, c + 1)])
                    add_neighbours(c, p, gin_masks[p])
            wait_apart(pe, [(act_evac, NC * K), (dve_evac, NC * K)])
            for p in range(KEPT):
                wait_apart(pe, [(y_second, NC)])
                add_neighbours(NC - 1, p, gin_masks[p])
                turn_x2_sums(p, p)
            gather(2, 0, gin_masks[2], (ring_landed, 16), layers(0) + layers(1), 1)
            gather(3, 1, gin_masks[3], (ring_landed, 32), layers(2), 2)
            with pe.Fori(0, (NC - 4) // 2) as i:
                gather(i * 2 + 4, 0, gin_masks[0], (mask_landed[0], i * 16 + 16), layers(i * 2 + 3), 2)
                gather(i * 2 + 5, 1, gin_masks[1], (mask_landed[1], i * 16 + 16), layers(i * 2 + 4), 2)
            for step in layers(NC - 1):
                step()

        @block.scalar
        def _(act):
            for g in range(NC):
                act.wait_ge(pe_pro, g + 1)
                act.activation(xT[:, g * CH:(g + 1) * CH], ps[:, g, :], ACT.Copy).then_inc(act_pro, 1)
            for g in range(NC):
                act.wait_ge(pe_pro, NC + g + 1)
                for half in range(2):
                    t = g * K + 2 * half
                    last = act.activation(
                        xw[:, t:t + 2, :],
                        ps[:, 2 * (g % 4) + half, :].rearrange("p (k n) -> p k n", k=2)[:, :, 0:F], ACT.Copy)
                last.then_inc(act_pro, 1)
            for g in range(NC):
                act.wait_ge(pe_pro, 2 * NC + g + 1)
                act.activation(s_rows[:, g * CH:(g + 1) * CH], ps[0:H, g, :], ACT.Copy).then_inc(act_pro, 1)
            act.wait_ge(act_pro, 3 * NC)
            act.dma_start(s_dram, s_rows).then_inc(s_stored, 16)
            act.wait_ge(exp_ready, 1)
            act.activation(vz[:, 0], ds[:, :, 0:H], ACT.Exp).then_inc(vz_ready, 1)
            act.activation(vz[:, 1], ds[:, :, 0:H], ACT.Exp, scale=SLOPE).then_inc(vz_ready, 1)
            act.wait_ge(exp_ready, 3)
            act.activation(uw[:, 0], uw[:, 0], ACT.Exp).then_inc(uw_ready, 1)
            act.activation(uw[:, 1], uw[:, 1], ACT.Exp, scale=-1.0).then_inc(uw_ready, 1)
            act.wait_ge(pe_pro, 3 * NC + 1)
            act.activation(wt[:].rearrange("p l n -> p (l n)"),
                           ps[:, 0:2, :].rearrange("p b n -> p (b n)"), ACT.Copy).then_inc(act_pro, 1)
            def greater(n, par, c, k, h):
                return act.activation(ringf8[:, c % RING, h, :, k], s_all[:, par, h, :], ACT.Relu,
                                      bias=dbig[:, c * K + k, h:h + 1], scale=STEP_GAIN, saturate=False)

            act.wait_ge(x2_scale, 1)
            act.activation(x2part[:, 0], x2raw, ACT.Copy, scale=x2top[:, 2:3]).then_inc(x2_first, 1)
            for j in range(2 * H):
                h, q = j // 2, j % 2
                act.wait_ge(den_cols, j + 1)
                act.wait_ge(part_ready, j + 1)
                act.activation(vz_part[:, :, 0, q, h, :], part[j % PARTS],
                               ACT.Copy).then_inc(first_ready, 1)
                if j >= 2:
                    if j == 2:
                        wait_apart(act, [s_there(0, 0)])
                    for k, h in steps[EARLY * (j - 2):EARLY * (j - 1)]:
                        greater(0, 0, 0, k, h)
            act.wait_ge(act_pro, 3 * NC + 1)

            def elu_exponential(n):
                act.wait_ge(neg_ready, n + 1)
                act.activation(neg, neg, ACT.Exp).then_inc(elu_exp, 1)

            def evacuate(n):
                wait(act, combined, n)
                for t in range(K):
                    act.wait_ge(acc_done, n * K + (t + 1))
                    act.activation(sums[:, t, 0:BANK0], ps[:, 2 * t, 0:BANK0],
                                   ACT.Copy).then_inc(act_evac, 1)

            def compare(n, par):
                first, second, final = (isinstance(n, int) and n == m for m in (0, 1, NC - 1))
                for c in range(NC):
                    m = n * NC + c
                    if first and c == 1:
                        act.wait_ge(second_ready, 2 * H)
                    if first and c == 2:
                        act.wait_ge(x2_second, 1)
                    if c == 0 and not (isinstance(n, int) and n < 2):
                        elu_exponential(n - 2)
                    if c == (2 if second else 3) and not first:
                        evacuate(n - 1)
                    counts = [(b_used, m + (1 - RING))]
                    if c == 0:
                        counts.append(s_there(n, par))
                    wait_apart(act, counts)
                    begin = EARLY * (2 * H - 2) if first and c == 0 else 0
                    for k, h in steps[begin:act_count(n, c)]:
                        last = greater(n, par, c, k, h)
                    last.then_inc(act_steps, 1)
                if final:
                    elu_exponential(n - 1)

            attention_chunks(act, compare)

            def root(made):
                act.wait_ge(var_ready, made)
                t = (made - 1) * (NT - K)
                act.activation(std[:, t:t + (NT - K if made == 1 else K)],
                               var[:, t:t + (NT - K if made == 1 else K)], ACT.Sqrt).then_inc(std_ready, 1)

            def y_first_part(c):
                act.wait_ge(y_ready, c + 1)
                act.activation(ypart[:, c, 0], xs[:, c * K:(c + 1) * K, :], ACT.Copy,
                               scale=Y_GAIN).then_inc(y_first, 1)

            root(1)
            for c in range(NC - 1):
                y_first_part(c)
            evacuate(NC - 1)
            act.wait_ge(neg_rest, 1)
            elu_exponential(NC - 1)
            root(2)
            y_first_part(NC - 1)

            def gin_layers(n, c, par):
                act.wait_ge(gin_done, n + 1)
                for q in range(2):
                    wait(act, merged, n)
                    act.activation(hid[:, 2 * q, :], ps[:, 2 * par + q, :], ACT.Copy,
                                   scale=gain[:, q:q + 1]).then_inc(hid_ready, 1)
                for l in range(L):
                    for q in range(2):
                        act.wait_ge(mlp_done, n * 2 * L + 2 * l + q + 1)
                        act.activation(hid[:, 2 * q + (l + 1) % 2, :], ps[:, 4 + q, :], ACT.Relu,
                                       bias=bias[:, q * L + l:q * L + l + 1]).then_inc(hid_ready, 1)
                act.wait_ge(o_var, n + 1)
                act.activation(std[:, 0:K], moments[:, :, 1], ACT.Sqrt,
                               bias=ln_eps[:, 0:1]).then_inc(o_std, 1)

            gin_chunks(act, gin_layers)

        @block.vector
        def _(dve):
            links = [0]

            def link(ins):
                links[0] += 1
                ins.then_inc(chain, 1)
                dve.wait_ge(chain, links[0])

            dve.wait_ge(w_landed, 32)
            wv = wext[:, 0:F].rearrange("p (h f) -> p h f", h=H)
            for q, at in ((1, F), (0, F + H)):
                link(dve.tensor_tensor(w_a, wv, a_all[:, :, q * FH:(q + 1) * FH], ALU.mult))
                last = dve.tensor_reduce(wext[:, at:at + H], w_a, X, ALU.add)
                if q == 1:
                    link(last)
            last.then_inc(wext_ready, 1)
            dve.memset(ln_eps[:], LN_EPS)
            dve.wait_ge(x2_landed, 16 * NB)
            dve.tensor_reduce(x2top[:, 0:1], x2raw.rearrange("p t f -> p (t f)"), X, ALU.max,
                              apply_absolute_value=True).then_inc(x2_top, 1)
            for g in range(NC):
                dve.wait_ge(act_pro, NC + g + 1)
                for half in range(2):
                    t = g * K + 2 * half
                    last = dve.tensor_copy(
                        ds[:, t:t + 2, :],
                        ps[:, 2 * (g % 4) + half, :].rearrange("p (k n) -> p k n", k=2)[:, :, F:F + 2 * H])
                last.then_inc(dve_pro, 1)
                dve.tensor_reduce(top_xw[:, g:g + 1], xw[:, g * K:(g + 1) * K, :].rearrange("p t f -> p (t f)"),
                                  X, ALU.max, apply_absolute_value=True).then_inc(xw_top, 1)
            dve.wait_ge(dve_pro, NC)
            dve.wait_ge(xw_top, NC)
            dve.tensor_reduce(top[:, H:H + 1], top_xw[:], X, ALU.max)
            dve.tensor_reduce(top[:, 0:H], ds[:, :, 0:H].rearrange("p t h -> p h t"), X,
                              ALU.max).then_inc(dve_pro, 1)
            dve.wait_ge(x2_topall, 1)
            link(dve.tensor_scalar(x2top[:, 1:2], x2top[:, 1:2], 1e-30, None, ALU.max))
            dve.tensor_scalar(x2top[:, 4:5], x2top[:, 1:2], 1.0 / (HP_TOP * MASK_ONE), None, ALU.mult)
            link(dve.tensor_scalar(x2top[:, 3:4], x2top[:, 1:2], 1.0 / HP_TOP, None, ALU.mult))
            dve.reciprocal(x2top[:, 2:3], x2top[:, 3:4]).then_inc(x2_scale, 1)
            dve.tensor_scalar(dneg[:], ds[:, :, 0:H], -1.0, None, ALU.mult)
            link(dve.tensor_scalar(dbig[:], ds[:, :, 0:H], STEP_GAIN, None, ALU.mult))

            def turn(n, par, t):
                s = n * K + t
                dve.wait_ge(adj_landed[t % 2], (n * 2 + (t // 2 + 1)) * 16 * NB)
                wait(dve, turned, s - 1)
                dve.tensor_scalar(mask[:, t % 2, :], rows[:, t % 2, :, :].rearrange("p b j -> p (b j)"),
                                  0.0, MASK_BYTE, ALU.is_gt, ALU.mult).then_inc(masked, 1)
                dve.wait_ge(masked, s + 1)
                dve.transpose(
                    maskT[:, par, :, t * P:(t + 1) * P].rearrange("p c (b i) -> p b c i", b=NB),
                    mask[:, t % 2, :].bitcast(I32).rearrange("p (b c w) -> p b c w", b=NB, w=Q)
                ).then_inc(turned, 1)

            dve.wait_ge(topall_ready, 1)
            dall = topall[:, 0:H].unsqueeze(1).to_broadcast([P, NT, H])
            link(dve.tensor_tensor(ds[:, :, H:2 * H], ds[:, :, H:2 * H], dall, ALU.add))
            dve.tensor_tensor(ds[:, :, 0:H], ds[:, :, 0:H], dall, ALU.subtract).then_inc(exp_ready, 1)
            dve.tensor_scalar(uw[:, 0], ds[:, :, H:2 * H], 1.0 - SLOPE, 0.0, ALU.mult,
                              ALU.min).then_inc(exp_ready, 1)
            dve.tensor_scalar(uw[:, 1], ds[:, :, H:2 * H], 1.0 - SLOPE, 0.0, ALU.mult,
                              ALU.max).then_inc(exp_ready, 1)
            link(dve.tensor_scalar(topall[:, H:H + 1], topall[:, H:H + 1], 1e-30, None, ALU.max))
            link(dve.reciprocal(hscale[:], topall[:, H:H + 1]))
            turn(0, 0, 0)
            dve.wait_ge(vz_ready, 2)
            link(dve.tensor_scalar(vz_den, vz, HP_TOP, None, ALU.mult))
            dve.tensor_scalar(vz, vz_den, hscale[:, 0:1], None, ALU.mult).then_inc(vz_scaled, 1)
            turn(0, 0, 1)
            dve.wait_ge(x2_first, 1)
            dve.scalar_tensor_tensor(out=x2part[:, 1], in0=x2raw, scalar=x2top[:, 2:3], in1=x2part[:, 0],
                                     op0=ALU.mult, op1=ALU.subtract).then_inc(x2_second, 1)
            for j in range(2 * H):
                h, q = j // 2, j % 2
                if j in (4, 6):
                    turn(0, 0, j // 2)
                dve.wait_ge(first_ready, j + 1)
                dve.tensor_tensor(vz_part[:, :, 1, q, h, :], part[j % PARTS], vz_part[:, :, 0, q, h, :],
                                  ALU.subtract).then_inc(second_ready, 1)

            def evacuate(n):
                wait(dve, combined, n)
                wait(dve, x2s_stored, n * 16)
                for t in range(K):
                    dve.wait_ge(acc_done, n * K + (t + 1))
                    dve.tensor_copy(sums[:, t, BANK0:ACC], ps[:, 2 * t + 1, 0:ACC - BANK0]).then_inc(dve_evac, 1)

            def reciprocals(n, tiles=tuple(range(K)), made=0):
                t0, t1 = tiles[0], tiles[-1] + 1
                dve.tensor_scalar(rden[:, t0:t1], full[:, t0:t1, :, 0, FH], hscale[:, 0:1], None,
                                  ALU.mult).then_inc(den_scaled, 1)
                dve.wait_ge(den_scaled, n + (1 + made))
                return dve.reciprocal(rden[:, t0:t1], rden[:, t0:t1])

            def row_statistics(n):
                for k in range(K):
                    last = dve.bn_stats(stats[:, bass.ds(n * K + k, 1), :].rearrange("p a s -> p (a s)"),
                                        xs[:, bass.ds(n * K + k, 1), :].rearrange("p a f -> p (a f)"))
                return last

            def mask_group(n, par, c):
                m = n * NC + c
                dve.wait_ge(act_steps, m + 1)
                dve.wait_ge(dve_steps, m + 1)
                dve.tensor_tensor(ring[:, c % RING], ring[:, c % RING],
                                  maskT[:, par, c:c + 1, :].to_broadcast([P, H, CH]),
                                  ALU.bitwise_and).then_inc(b_ready, 1)

            def compare(n, par):
                first, second, final = (isinstance(n, int) and n == m for m in (0, 1, NC - 1))
                for c in range(NC):
                    m = n * NC + c
                    if first and c == 2:
                        dve.wait_ge(x2_second, 1)
                    if c == (2 if second else 3) and not first:
                        evacuate(n - 1)
                    wait(dve, b_used, m + (1 - RING))
                    if c == 0:
                        dve.wait_ge(*s_there(n, par))
                        dve.wait_ge(turned, n * K + K)
                    if first and c == 0:
                        dve.sem_inc(dve_steps, 1)
                    else:
                        for k, h in steps[act_count(n, c):]:
                            last = dve.tensor_scalar(
                                ring8[:, c % RING, h, :, k], s_all[:, par, h, :],
                                dneg[:, c * K + k, h:h + 1], MASK_BYTE, ALU.is_gt, ALU.mult)
                        last.then_inc(dve_steps, 1)
                    if c > 0:
                        mask_group(n, par, c - 1)
                    if c == 1 and not (isinstance(n, int) and n < 2):
                        dve.wait_ge(combined, n - 1)
                        row_statistics(n - 2).then_inc(stats_ready, 1)
                    if c == 6 and not first:
                        dve.wait_ge(den_ready, n)
                        reciprocals(n - 1).then_inc(rden_ready, 1)
                    if c >= NC - K and not final:
                        if c == NC - K:
                            wait(dve, acc_done, n * K)
                            wait(dve, mask_stored, n * 16)
                        turn(n + 1, 1 - par, c - (NC - K))
                mask_group(n, par, NC - 1)
                if final:
                    dve.wait_ge(combined, n)
                    row_statistics(n - 1).then_inc(stats_ready, 1)

            dve.wait_ge(second_ready, 2 * H)
            attention_chunks(dve, compare)

            def row_moments(t0, t1):
                mm, dd, vv = mean[:, t0:t1], spread[:, t0:t1], var[:, t0:t1]
                dve.tensor_tensor(mm, stats[:, t0:t1, 1], stats[:, t0:t1, 4], ALU.add)
                dve.tensor_tensor(dd, stats[:, t0:t1, 1], stats[:, t0:t1, 4], ALU.subtract)
                link(dve.tensor_tensor(vv, stats[:, t0:t1, 2], stats[:, t0:t1, 5], ALU.add))
                dve.tensor_scalar(mm, mm, 0.5, None, ALU.mult)
                dve.tensor_tensor(dd, dd, dd, ALU.mult)
                link(dve.tensor_scalar(vv, vv, 1.0 / F, LN_EPS, ALU.mult, ALU.add))
                dve.scalar_tensor_tensor(out=vv, in0=dd, scalar=0.25, in1=vv, op0=ALU.mult,
                                         op1=ALU.add).then_inc(var_ready, 1)

            def y_rows(c):
                for t in range(c * K, (c + 1) * K):
                    last = dve.tensor_scalar(xs[:, t, :], xs[:, t, :], mean[:, t:t + 1], rstd[:, t:t + 1],
                                             ALU.subtract, ALU.mult)
                last.then_inc(y_ready, 1)

            def y_rest(c):
                dve.wait_ge(y_first, c + 1)
                dve.scalar_tensor_tensor(out=ypart[:, c, 1], in0=xs[:, c * K:(c + 1) * K, :], scalar=Y_GAIN,
                                         in1=ypart[:, c, 0], op0=ALU.mult,
                                         op1=ALU.subtract).then_inc(y_second, 1)

            dve.wait_ge(stats_ready, NC - 1)
            row_moments(0, NT - K)
            dve.wait_ge(gin_w_landed, 16 * (2 * L + 6))
            dve.tensor_scalar(gain[:, 0:1], eps_all[:, 0:1], 2.0, 1.0 / (Y_GAIN * MASK_ONE), ALU.add, ALU.mult)
            dve.tensor_scalar(gain[:, 1:2], eps_all[:, 1:2], 2.0, x2top[:, 4:5], ALU.add, ALU.mult)
            dve.wait_ge(std_ready, 1)
            link(dve.reciprocal(rstd[:, 0:NT - K], std[:, 0:NT - K]))
            for c in range(NC - 1):
                y_rows(c)
                if c > 0:
                    y_rest(c - 1)
            y_rest(NC - 2)
            evacuate(NC - 1)

            dve.wait_ge(act_evac, NC * K)
            dve.wait_ge(dve_evac, NC * K)
            dve.wait_ge(uw_ready, 2)
            tiles = dve_tiles
            t0, t1 = tiles[0], K
            link(combine_sums(dve, NC - 1, tiles, link))
            link(reciprocals(NC - 1, tiles))
            link(attention_output(dve, NC - 1, tiles))
            dve.wait_ge(den_ready, NC)
            reciprocals(NC - 1, pool_tiles, 1).then_inc(rden_ready, 1)
            dve.tensor_scalar(neg[:, t0:t1], g_out[:, t0:t1], 0.0, None,
                              ALU.min).then_inc(neg_rest, 1)
            link(dve.tensor_scalar(g_out[:, t0:t1], g_out[:, t0:t1], 0.0, -1.0,
                                   ALU.max, ALU.add))
            link(dve.tensor_tensor(rows_of(xs, NC - 1, tiles), rows_of(xs, NC - 1, tiles),
                                   g_out[:, t0:t1], ALU.add))
            dve.wait_ge(elu_exp, NC)
            link(dve.tensor_tensor(rows_of(xs, NC - 1, tiles), rows_of(xs, NC - 1, tiles),
                                   neg[:, t0:t1], ALU.add))
            dve.wait_ge(combined, NC)
            row_statistics(NC - 1).then_inc(stats_ready, 1)
            dve.wait_ge(stats_ready, NC)
            row_moments(NT - K, NT)
            dve.wait_ge(std_ready, 2)
            link(dve.reciprocal(rstd[:, NT - K:NT], std[:, NT - K:NT]))
            y_rows(NC - 1)
            y_rest(NC - 1)
            dve.wait_ge(y_second, NC)
            link(dve.tensor_tensor(xs[:], xs[:], bm_all[:].unsqueeze(1).to_broadcast([P, NT, F]), ALU.add))

            def finish(n, c, par):
                cen, o = res[:, 0], res[:, 2]
                base = links[0]
                wait(dve, o_ready, n)
                dve.wait_ge(merged, n + 1)
                dve.tensor_tensor(cen, ps[:, 6, :].rearrange("p (k f) -> p k f", k=K),
                                  xs[:, bass.ds(c * K, K), :], ALU.add).then_inc(sum_ready, 1)
                dve.wait_ge(sum_ready, n + 1)
                for k in range(K):
                    last = dve.bn_stats(stats[:, k, :], cen[:, k, :])
                last.then_inc(chain, 1)
                wait_apart(dve, [(chain, n * 2 + (base + 1))])
                for k in range(K):
                    last = dve.bn_aggr(moments[:, k, :], stats[:, k, :])
                last.then_inc(o_var, 1)
                dve.wait_ge(o_std, n + 1)
                dve.reciprocal(rstd[:, 0:K], std[:, 0:K]).then_inc(chain, 1)
                dve.wait_ge(chain, n * 2 + (base + 2))
                wait(dve, out_stored, n * (16 * NB))
                for k in range(K):
                    last = dve.tensor_scalar(o[:, k, :], cen[:, k, :], moments[:, k, 0:1], rstd[:, k:k + 1],
                                             ALU.subtract, ALU.mult)
                last.then_inc(o_ready, 1)

            gin_chunks(dve, finish)


_INS = ['x', 'adj', 'L0_gnn_W', 'L0_gnn_a', 'L1_gnn_x2', 'L1_gnn_eps1', 'L1_gnn_eps2', 'L1_gnn_W1',
        'L1_gnn_b1', 'L1_gnn_W2', 'L1_gnn_b2', 'L1_gnn_Wm', 'L1_gnn_bm']
_OUTS = [((4096, 128), 'float32')]


def kernel(**inputs):
    import numpy as _np
    import concourse.bacc as _bacc
    from concourse import mybir as _mybir
    from concourse.bass_utils import run_bass_kernel_spmd as _run

    nc = _bacc.Bacc("TRN2", target_bir_lowering=False, num_devices=1)
    arrays, args = {}, []
    for name in _INS:
        a = _np.ascontiguousarray(inputs[name])
        arrays[f"in_{name}_dram"] = a
        args.append(nc.dram_tensor(f"in_{name}_dram", a.shape, _mybir.dt.from_np(a.dtype), kind="ExternalInput").ap())
    for i, (shape, dtype) in enumerate(_OUTS):
        dt = _mybir.dt.from_np(_np.dtype(dtype))
        args.append(nc.dram_tensor(f"out_{i}_dram", shape, dt, kind="ExternalOutput").ap())
    gat_gin_resnorm_kernel(nc, *args)
    r = _run(nc, [arrays], core_ids=[0])
    got = tuple(r.results[0][f"out_{i}_dram"] for i in range(len(_OUTS)))
    return got[0]
```
